# Optimizing a Trainium2 kernel written in Bass

```python
import numpy as np
import jax
import jax.numpy as jnp

def _softmax(x, axis=-1):
    return jax.nn.softmax(x, axis=axis)

def _gelu(x):
    return jax.nn.gelu(x, approximate=True)

def _silu(x):
    return jax.nn.silu(x)

def _sigmoid(x):
    return jax.nn.sigmoid(x)

def _layernorm(x, axis=-1, eps=1e-05):
    m = jnp.mean(x, axis=axis, keepdims=True)
    v = jnp.var(x, axis=axis, keepdims=True)
    return (x - m) / jnp.sqrt(v + eps)

def _scatter_add(tgt, idx, src, axis=0):
    return tgt.at[idx].add(src)

def _segment_sum(src, seg, n):
    return jax.ops.segment_sum(src, seg, n)
kernel_name = 'mk_gnn_resnorm_d2_gnn_r64_671b18'

def setup_inputs(seed: int=0):
    np.random.seed(seed)
    _w = jnp.asarray

    def _rec_inputs():
        import jax
        import jax.numpy as jnp
        _gk = jax.random.key(seed)
        x = -0.000202 + 1 * jax.random.normal(jax.random.fold_in(_gk, 1), (50000, 128), jnp.float32)
        src = jax.random.randint(jax.random.fold_in(_gk, 2), (25000,), 0, 50000, jnp.int32)
        dst = jax.random.randint(jax.random.fold_in(_gk, 3), (25000,), 0, 50000, jnp.int32)
        _o = jnp.argsort(dst, stable=True)
        src = src[_o]
        dst = dst[_o]
        edge_attr_128 = -5.16925e-05 + 1.00005 * jax.random.normal(jax.random.fold_in(_gk, 12), (25000, 128), jnp.float32)
        edge_weight = 0.000614103 + 0.999867 * jax.random.normal(jax.random.fold_in(_gk, 14), (25000,), jnp.float32)
        return (x, src, dst, edge_attr_128, edge_weight)
    x, src, dst, edge_attr_128, edge_weight = _rec_inputs()

    def _L0_gnn_setup():
        import jax, jax.numpy as jnp
        import numpy as np
        N, E, D, G, L = (50000, 12500, 128, 50, 3)
        LN_EPS = 1e-05

        def _ln(x, w, b):
            mu = x.mean(-1, keepdims=True)
            var = ((x - mu) ** 2).mean(-1, keepdims=True)
            return (x - mu) / jnp.sqrt(var + LN_EPS) * w + b

        def _graph_norm(x, batch, w, b, num_graphs):
            F = x.shape[-1]
            cnt = jax.ops.segment_sum(jnp.ones((x.shape[0],), x.dtype), batch, num_segments=num_graphs)
            norm = jnp.maximum(cnt, 1.0) * F
            mean = jax.ops.segment_sum(x, batch, num_segments=num_graphs).sum(-1) / norm
            xc = x - mean[batch][:, None]
            var = jax.ops.segment_sum(xc * xc, batch, num_segments=num_graphs).sum(-1) / norm
            out = xc / jnp.sqrt(var + LN_EPS)[batch][:, None]
            return out * w + b
        key = jax.random.key(seed)
        ks = jax.random.split(key, 8)
        node = jax.random.normal(ks[0], (N, D), dtype=jnp.float32)
        edge_index = jax.random.randint(ks[1], (2, E), 0, N, dtype=jnp.int64)
        edge_attr = jax.random.normal(ks[2], (E,), dtype=jnp.float32)
        batch = jnp.sort(jax.random.randint(ks[3], (N,), 0, G, dtype=jnp.int64))
        scale = 1.0 / np.sqrt(D)
        W = jax.random.normal(ks[4], (L, 3, D, D), dtype=jnp.float32) * scale
        b = jax.random.normal(ks[5], (L, 3, D), dtype=jnp.float32) * scale
        mlp_ln_w = jnp.ones((L, 2, D), jnp.float32)
        mlp_ln_b = jnp.zeros((L, 2, D), jnp.float32)
        eps = jnp.zeros((L,), jnp.float32)
        out_ln_w = jnp.ones((L, D), jnp.float32)
        out_ln_b = jnp.zeros((L, D), jnp.float32)
        return {'node': node, 'edge_index': edge_index, 'edge_attr': edge_attr, 'batch': batch, 'W': W, 'b': b, 'mlp_ln_w': mlp_ln_w, 'mlp_ln_b': mlp_ln_b, 'eps': eps, 'out_ln_w': out_ln_w, 'out_ln_b': out_ln_b}
    _L0_gnn_all = _L0_gnn_setup()
    _L0_gnn_in = {k: v for k, v in _L0_gnn_all.items() if k in ('W', 'b', 'mlp_ln_w', 'mlp_ln_b', 'eps', 'out_ln_w', 'out_ln_b')}
    del _L0_gnn_all

    def _L1_gnn_setup():
        import jax, jax.numpy as jnp
        import numpy as np
        N, E, D = (50000, 12500, 128)
        LN_EPS = 1e-05
        key = jax.random.key(seed)
        ks = jax.random.split(key, 8)
        x = jax.random.normal(ks[0], (N, D), dtype=jnp.float32)
        edge_index = jax.random.randint(ks[1], (2, E), 0, N, dtype=jnp.int64)
        edge_attr = jax.random.normal(ks[2], (E, D), dtype=jnp.float32)
        s_msg = 1.0 / np.sqrt(2 * D)
        s_upd = 1.0 / np.sqrt(2 * D)
        W_msg = jax.random.uniform(ks[3], (2 * D, D), jnp.float32, -s_msg, s_msg)
        b_msg = jax.random.uniform(ks[4], (D,), jnp.float32, -s_msg, s_msg)
        W_upd = jax.random.uniform(ks[5], (2 * D, D), jnp.float32, -s_upd, s_upd)
        b_upd = jax.random.uniform(ks[6], (D,), jnp.float32, -s_upd, s_upd)
        gamma = jnp.ones((D,), jnp.float32)
        beta = jnp.zeros((D,), jnp.float32)
        return {'x': x, 'edge_index': edge_index, 'edge_attr': edge_attr, 'W_msg': W_msg, 'b_msg': b_msg, 'W_upd': W_upd, 'b_upd': b_upd, 'gamma': gamma, 'beta': beta}
    _L1_gnn_all = _L1_gnn_setup()
    _L1_gnn_in = {k: v for k, v in _L1_gnn_all.items() if k in ('W_msg', 'b_msg', 'W_upd', 'b_upd', 'gamma', 'beta')}
    del _L1_gnn_all
    return {'x': x, 'src': src, 'dst': dst, 'edge_attr_128': edge_attr_128, 'edge_weight': edge_weight, 'L0_gnn_W': _L0_gnn_in['W'], 'L0_gnn_b': _L0_gnn_in['b'], 'L0_gnn_mlp_ln_w': _L0_gnn_in['mlp_ln_w'], 'L0_gnn_mlp_ln_b': _L0_gnn_in['mlp_ln_b'], 'L0_gnn_eps': _L0_gnn_in['eps'], 'L0_gnn_out_ln_w': _L0_gnn_in['out_ln_w'], 'L0_gnn_out_ln_b': _L0_gnn_in['out_ln_b'], 'L1_gnn_W_msg': _L1_gnn_in['W_msg'], 'L1_gnn_b_msg': _L1_gnn_in['b_msg'], 'L1_gnn_W_upd': _L1_gnn_in['W_upd'], 'L1_gnn_b_upd': _L1_gnn_in['b_upd'], 'L1_gnn_gamma': _L1_gnn_in['gamma'], 'L1_gnn_beta': _L1_gnn_in['beta']}

def reference(x, src, dst, edge_attr_128, edge_weight, L0_gnn_W, L0_gnn_b, L0_gnn_mlp_ln_w, L0_gnn_mlp_ln_b, L0_gnn_eps, L0_gnn_out_ln_w, L0_gnn_out_ln_b, L1_gnn_W_msg, L1_gnn_b_msg, L1_gnn_W_upd, L1_gnn_b_upd, L1_gnn_gamma, L1_gnn_beta):
    import jax
    import jax.numpy as jnp

    def _L0_gnn_ref(node, edge_index, edge_attr, batch, W, b, mlp_ln_w, mlp_ln_b, eps, out_ln_w, out_ln_b):
        import jax, jax.numpy as jnp
        import numpy as np
        N, E, D, G, L = (50000, 12500, 128, 50, 3)
        LN_EPS = 1e-05

        def _ln(x, w, b):
            mu = x.mean(-1, keepdims=True)
            var = ((x - mu) ** 2).mean(-1, keepdims=True)
            return (x - mu) / jnp.sqrt(var + LN_EPS) * w + b

        def _graph_norm(x, batch, w, b, num_graphs):
            F = x.shape[-1]
            cnt = jax.ops.segment_sum(jnp.ones((x.shape[0],), x.dtype), batch, num_segments=num_graphs)
            norm = jnp.maximum(cnt, 1.0) * F
            mean = jax.ops.segment_sum(x, batch, num_segments=num_graphs).sum(-1) / norm
            xc = x - mean[batch][:, None]
            var = jax.ops.segment_sum(xc * xc, batch, num_segments=num_graphs).sum(-1) / norm
            out = xc / jnp.sqrt(var + LN_EPS)[batch][:, None]
            return out * w + b
        src, dst = (edge_index[0], edge_index[1])
        x = node
        for l in range(L):
            agg = jnp.zeros_like(x).at[dst].add(x[src])
            h = (1.0 + eps[l]) * x + agg
            for i in range(3):
                h = h @ W[l, i].T + b[l, i]
                if i < 2:
                    h = jax.nn.relu(_ln(h, mlp_ln_w[l, i], mlp_ln_b[l, i]))
            x = jax.nn.relu(_graph_norm(h, batch, out_ln_w[l], out_ln_b[l], G))
        return x

    def _L1_gnn_ref(x, edge_index, edge_attr, W_msg, b_msg, W_upd, b_upd, gamma, beta):
        import jax, jax.numpy as jnp
        import numpy as np
        N, E, D = (50000, 12500, 128)
        LN_EPS = 1e-05
        src, dst = (edge_index[0], edge_index[1])
        n = x.shape[0]
        msg_in = jnp.concatenate([x[src], edge_attr], axis=-1)
        msg = jax.nn.relu(msg_in @ W_msg + b_msg)
        summed = jax.ops.segment_sum(msg, dst, num_segments=n)
        counts = jax.ops.segment_sum(jnp.ones((msg.shape[0],), x.dtype), dst, num_segments=n)
        mean_msg = summed / jnp.maximum(counts, 1.0)[:, None]
        h = jnp.concatenate([x, mean_msg], axis=-1) @ W_upd + b_upd
        mu = jnp.mean(h, axis=-1, keepdims=True)
        var = jnp.mean(jnp.square(h - mu), axis=-1, keepdims=True)
        h = (h - mu) * jax.lax.rsqrt(var + LN_EPS) * gamma + beta
        return jax.nn.relu(h + x)
    edge_index = jnp.stack([src, dst])
    batch0 = jnp.zeros((50000,), jnp.int32)
    x = _layernorm(x + _L0_gnn_ref(x, edge_index, edge_weight, batch0, L0_gnn_W, L0_gnn_b, L0_gnn_mlp_ln_w, L0_gnn_mlp_ln_b, L0_gnn_eps, L0_gnn_out_ln_w, L0_gnn_out_ln_b), axis=-1)
    x = _layernorm(x + _L1_gnn_ref(x, edge_index, edge_attr_128, L1_gnn_W_msg, L1_gnn_b_msg, L1_gnn_W_upd, L1_gnn_b_upd, L1_gnn_gamma, L1_gnn_beta), axis=-1)
    return x

_drawn_inputs = setup_inputs


def setup_inputs(seed=0):
    import zlib

    import numpy as np

    out = dict(_drawn_inputs(seed))
    spreads = {'L0_gnn_mlp_ln_w': (1.0, 0.2),
     'L0_gnn_mlp_ln_b': (0.0, 0.1),
     'L0_gnn_eps': (0.0, 0.8),
     'L0_gnn_out_ln_w': (1.0, 0.2),
     'L0_gnn_out_ln_b': (0.0, 0.1),
     'L1_gnn_gamma': (1.0, 0.2),
     'L1_gnn_beta': (0.0, 0.1)}
    factors = {'L1_gnn_b_msg': 8.0}
    for name, (base, spread) in spreads.items():
        noise = np.random.default_rng([zlib.crc32(name.encode()), seed]).standard_normal(out[name].shape)
        drawn = base * np.exp(spread * noise) if base else spread * noise
        out[name] = jnp.asarray(drawn.astype(out[name].dtype))
    for name, factor in factors.items():
        out[name] = (out[name] * factor).astype(out[name].dtype)
    return out
```

```python
from contextlib import ExitStack

import concourse.bass as bass
from concourse import mybir

F32 = mybir.dt.float32
BF16 = mybir.dt.bfloat16
I32 = mybir.dt.int32
U8 = mybir.dt.uint8
ALU = mybir.AluOpType
ACT = mybir.ActivationFunctionType
AXX = mybir.AxisListType.X

N, E, D, LAYERS = 50000, 25000, 128, 3
P = 128
TILES = 4
ROWS = P * TILES
CHUNKS = -(-N // ROWS)
NPAD = CHUNKS * ROWS
TAIL = (N - (CHUNKS - 1) * ROWS) // TILES
ECHUNKS = -(-E // ROWS)
EPAD = ECHUNKS * ROWS
ETILES = EPAD // P
HALF = ETILES // 2
FULLROWS = E // P - HALF
REST = E % P
NOWHERE = 1 << 20
EPS = 1e-5
STATGROUP = ROWS // 2
EVEN = [(ECHUNKS + 1) // 2, ECHUNKS // 2]
PAIRS = CHUNKS // 2


class Chunk:

    def __init__(self, n, half, const, fixed):
        self.n, self.half, self.q, self.q4, self.fixed = n, half, const % 2, const % 4, fixed

    def is_(self, value):
        return self.fixed and self.n == value


def sweep(eng, count, stages, unroll=2):
    deepest = max(lag for lag, _ in stages)
    lead = -(-(deepest + 2) // unroll) * unroll
    blocks = (count - 1) // unroll

    def peeled(t):
        for lag, stage in stages:
            c = t - lag
            if 0 <= c < count:
                stage(Chunk(c, c // 2, c, True))

    for t in range(lead):
        peeled(t)
    with eng.Fori(lead // unroll, blocks) as k:
        for r in range(unroll):
            for lag, stage in stages:
                const = r - lag
                stage(Chunk(k * unroll + const, k * (unroll // 2) + const // 2, const, False))
    for t in range(blocks * unroll, count + deepest):
        peeled(t)


def wait(eng, sem, value):
    if isinstance(value, int) and value <= 0:
        return
    eng.wait_ge(sem, value)


def build(nc, x, src, dst, edge_attr_128, L0_gnn_W, L0_gnn_b, L0_gnn_mlp_ln_w, L0_gnn_mlp_ln_b,
          L0_gnn_eps, L0_gnn_out_ln_w, L0_gnn_out_ln_b, L1_gnn_W_msg, L1_gnn_b_msg, L1_gnn_W_upd,
          L1_gnn_b_upd, L1_gnn_gamma, L1_gnn_beta, out):
    ctx = ExitStack()
    with ctx:
        def sb(name, shape, dt=F32):
            return ctx.enter_context(nc.sbuf_tensor(name, shape, dt))

        def sem(name):
            return ctx.enter_context(nc.semaphore(name))

        def sems(name, n=2):
            return [sem(f"{name}{i}") for i in range(n)]

        act_rows = nc.dram_tensor("act_rows", [NPAD, D], F32).ap()
        x1_rows = nc.dram_tensor("x1_rows", [NPAD, D], F32).ap()
        agg = nc.dram_tensor("agg", [NPAD, D], F32).ap()
        attr_rows = nc.dram_tensor("attr_rows", [EPAD, D], F32).ap()
        same_row = nc.dram_tensor("same_row", [1, EPAD + 1], U8).ap()

        def chunks_of(t):
            return t.rearrange("(c p j) f -> c p (j f)", p=P, j=TILES)

        act_c, x1_c, agg_c = chunks_of(act_rows), chunks_of(x1_rows), chunks_of(agg)
        WHOLE = (CHUNKS - 1) * ROWS
        x_c = chunks_of(x[0:WHOLE, :])
        x_tail = x[WHOLE:N, :].rearrange("(p j) f -> p (j f)", j=TILES)
        out_c = chunks_of(out[0:WHOLE, :])
        out_tail = out[WHOLE:N, :].rearrange("(p j) f -> p (j f)", j=TILES)
        attr_c = attr_rows.rearrange("(c j p) f -> c p j f", j=TILES, p=P)

        ident = sb("ident", [P, P])
        ones = sb("ones", [P, P])
        pick = sb("pick", [P, P], BF16)
        zeros = sb("zeros", [P, 1568])
        onerow = sb("onerow", [P, ROWS], BF16)
        linT = sb("linT", [P, 9, D])
        w_msg = sb("w_msg", [P, 2, D])
        w_upd = sb("w_upd", [P, 2, D])
        bias3 = sb("bias3", [P, 10, D], BF16)
        cols = sb("cols", [P, P])
        eps1 = sb("eps1", [P, LAYERS])
        epsc = sb("epsc", [P, 1])
        src_tab = sb("src_tab", [P, ETILES], I32)
        end_tab = sb("end_tab", [P, ETILES], I32)
        same = sb("same", [P, EPAD], U8)
        need_row = sb("need_row", [1, CHUNKS], I32)
        sums = sb("sums", [P, ECHUNKS, ROWS])
        h_in = sb("h_in", [P, 2, ROWS])
        a_in = sb("a_in", [P, 2, ROWS])
        work = sb("work", [P, 22, ROWS])
        sum_out = sb("sum_out", [P, 2, ROWS])
        src_now = sb("src_now", [P, 2, TILES], I32)
        end_now = sb("end_now", [P, 2, TILES], I32)
        st1 = sb("st1", [P, 2, TILES, 6])
        st2 = sb("st2", [P, 2, TILES, 6])
        var1 = sb("var1", [P, 2, TILES])
        var2 = sb("var2", [P, 2, TILES])
        part1 = sb("part1", [P, 2, 4, TILES])
        part2 = sb("part2", [P, 2, 4, TILES])
        mean1 = sb("mean1", [P, 2, TILES])
        mean2 = sb("mean2", [P, 2, TILES])
        sd1 = sb("sd1", [P, 2, TILES])
        sd2 = sb("sd2", [P, 2, TILES])
        r1 = sb("r1", [P, 2, TILES])
        r2 = sb("r2", [P, 2, TILES])
        st3 = sb("st3", [P, CHUNKS, 6])
        dev = sb("dev", [P, CHUNKS, 2])
        valid = sb("valid", [P, 1])
        tot = sb("tot", [P, 8])
        gn_scale = sb("gn_scale", [P, LAYERS])
        gn_bias = sb("gn_bias", [P, LAYERS])

        def ring(first, n=2):
            return [work[:, first + i, :] for i in range(n)]

        xT, h0T, n1, h1T, n2, h2T, o_rows = (ring(2 * i) for i in range(7))
        gathered, gT, yT = ring(4), ring(6), ring(8)
        attr_in, attrT, msgT, meanT, count, inv = (ring(2 * i) for i in (5, 6, 7, 8, 9, 10))
        x_in, z1 = ring(14), ring(16)
        x1T, meanT4, n4, u4, v4, x1_in, z4, out_rows = (
            ring(0, 4), ring(4), ring(6), ring(8), ring(10), ring(12), ring(14), ring(16))

        idx_rows = work[:, 0:2, :].rearrange("p a b -> p (a b)").bitcast(I32)
        idx_f = work[:, 2:4, :].rearrange("p a b -> p (a b)")
        w_rows = work[:, 4:7, :].rearrange("p a b -> p (a b)")[:, 0:9 * D]
        b_rows = work[:, 7:10, :].rearrange("p a b -> p (a b)")[:, 0:10 * D]
        b_part = work[:, 10:13, :].rearrange("p a b -> p (a b)")[:, 0:10 * D]
        v_rows = work[:, 13, 0:P]
        thr_i = work[:, 14, 0:CHUNKS].bitcast(I32)
        thr = work[:, 14, P:P + CHUNKS]
        reach = work[:, 15, 0:2 * P]
        b_bf = work[:, 16:18, :].rearrange("p a b -> p (a b)").bitcast(BF16)[:, 0:10 * D]
        means9 = work[:, 18, 0:32]
        same_rows = work[:, 19, 0:64].bitcast(U8)

        def idx_block(t, k):
            return t[:, k * 2 * P:(k + 1) * 2 * P].rearrange("p (u e) -> p u e", u=2)

        src_i, dst_i, nxt_i = (idx_block(idx_rows, k) for k in range(3))
        src_f, dst_f, nxt_f, end_f = (idx_block(idx_f, k) for k in range(4))

        bank = [ctx.enter_context(nc.psum_tensor(f"bank{i}", [P, ROWS], F32)) for i in range(8)]
        b_x, b_a, b_t1, b_2, b_t2, b_3 = bank[0], bank[1], bank[2], bank[3], bank[4], bank[5]
        b_1 = [bank[6], bank[7]]

        LNW, LNB, OW, OB, GAM, BET, BMSG = 0, 6, 12, 15, 18, 19, 20

        def col(i):
            return cols[:, i:i + 1]

        def tiles(ap):
            return ap.rearrange("p (j f) -> p j f", j=TILES)

        def tile(ap, j):
            return ap[:, j * P:(j + 1) * P]

        s_consts, s_fill, s_idx, s_params, s_same_out, s_same_in = (
            sem(n) for n in ("consts", "filled", "idx_loaded", "params_loaded", "same_stored", "same_loaded"))
        s_setup_dve, s_setup_pe, s_setup_act = sem("setup_dve"), sem("setup_pe"), sem("setup_act")
        s_zeroed, s_attr_copied = sem("agg_zeroed"), sem("attr_copied")
        s_src_now, s_end_now, s_tick = sem("src_now_set"), sem("end_now_set"), sem("pool_tick")
        s_gath = sems("rows_gathered")
        s_scat = sems("rows_scattered")
        s_scattered = sem("tiles_scattered")
        e_gT_psum, e_gT, e_scan, e_yT_psum, e_y = (
            sem(n) for n in ("edge_rows_turned", "edge_gT", "edge_scanned", "edge_sums_turned", "edge_sums_kept"))
        s_hload, s_aload, s_store = sems("h_loaded"), sems("a_loaded"), sems("rows_stored")
        d_turned, d_xT, d_h0, d_mm1, d_st1, d_var1, d_sd1, d_r1, d_n1, d_n1T, d_h1 = (
            sem(n) for n in ("d_turned", "d_xT", "d_h0", "d_mm1", "d_st1", "d_var1", "d_sd1", "d_r1", "d_n1",
                             "d_n1T", "d_h1"))
        d_mm2, d_st2, d_var2, d_sd2, d_r2, d_n2, d_n2T, d_h2, d_mm3, d_o, d_ost = (
            sem(n) for n in ("d_mm2", "d_st2", "d_var2", "d_sd2", "d_r2", "d_n2", "d_n2T", "d_h2", "d_mm3", "d_o",
                             "d_ost"))
        d_part1, d_part2, y_part, f_part1, f_part2 = (sem(n) for n in ("d_part1", "d_part2", "y_part", "f_part1", "f_part2"))
        s_chain, s_total_pe, s_total_act, s_gn = (
            sem(n) for n in ("dve_chain", "total_pe", "total_act", "graph_norm_ready"))
        y_hload, y_xload, y_store = sems("y_h_loaded"), sems("y_x_loaded"), sems("x1_stored")
        y_turned, y_xT, y_back, y_z, y_st, y_var, y_sd, y_r, y_o = (
            sem(n) for n in ("y_turned", "y_xT", "y_back", "y_z", "y_st", "y_var", "y_sd", "y_r", "y_o"))
        m_attr = sems("attr_loaded")
        m_gT_psum, m_aT_psum, m_gT, m_aT, m_mm, m_msg, m_scan, m_cnt, m_inv, m_mean, m_yT_psum, m_y = (
            sem(n) for n in ("m_gT_psum", "m_aT_psum", "m_gT", "m_aT", "m_mm", "m_msg", "m_scan", "m_cnt", "m_inv",
                             "m_mean", "m_yT_psum", "m_y"))
        f_hload, f_aload, f_xload, f_store = (
            sems("f_h_loaded"), sems("f_a_loaded"), sems("f_x_loaded"), sems("out_stored"))
        (f_turned, f_xT, f_aT, f_mm, f_st1, f_var1, f_sd1, f_r1, f_n1, f_n1T, f_u, f_v, f_vT, f_z, f_st2, f_var2,
         f_sd2, f_r2, f_o) = (
            sem("f_" + n) for n in ("turned", "xT", "aT", "mm", "st1", "var1", "sd1", "r1", "n1", "n1T", "u", "v",
                                    "vT", "z", "st2", "var2", "sd2", "r2", "o"))
        N_PARAMS = 13
        ZERO_PIECES = NPAD * D // P // zeros.shape[1]

        block = ctx.enter_context(nc.Block())

        @block.sync
        def _(sp):
            sp.wait_ge(s_fill, 1)
            for table, rows, shift in ((src, src_i, 0), (dst, dst_i, 0), (dst, nxt_i, 1)):
                first = HALF * P
                second = FULLROWS * P
                sp.dma_start(rows[0:HALF, 0, :],
                             table[shift:shift + first].rearrange("(t e) -> t e", e=P)).then_inc(s_idx, 16)
                sp.dma_start(rows[0:FULLROWS, 1, :],
                             table[shift + first:shift + first + second].rearrange("(t e) -> t e", e=P)
                             ).then_inc(s_idx, 16)
                sp.dma_start(rows[FULLROWS:FULLROWS + 1, 1, 0:REST - shift],
                             table[shift + first + second:E].unsqueeze(0)).then_inc(s_idx, 16)
            sp.wait_ge(s_consts, 6)
            sp.dma_start(w_rows.rearrange("p (m k) -> p m k", k=D),
                         L0_gnn_W.rearrange("l i o k -> o (l i) k")).then_inc(s_params, 16)
            sp.dma_start(b_rows[:, 0:9 * D],
                         L0_gnn_b.rearrange("l i o -> (l i o)").partition_broadcast(P)).then_inc(s_params, 16)
            sp.dma_start(b_rows[:, 9 * D:10 * D], L1_gnn_b_upd.partition_broadcast(P)).then_inc(s_params, 16)
            sp.dma_start(w_msg[:, :, :], L1_gnn_W_msg.rearrange("(h k) f -> k h f", k=P)).then_inc(s_params, 16)
            sp.dma_start(w_upd[:, :, :], L1_gnn_W_upd.rearrange("(h k) f -> k h f", k=P)).then_inc(s_params, 16)
            for at, rows in ((LNW, L0_gnn_mlp_ln_w.rearrange("l i f -> (l i) f")),
                             (LNB, L0_gnn_mlp_ln_b.rearrange("l i f -> (l i) f")),
                             (OW, L0_gnn_out_ln_w), (OB, L0_gnn_out_ln_b), (GAM, L1_gnn_gamma.unsqueeze(0)),
                             (BET, L1_gnn_beta.unsqueeze(0)), (BMSG, L1_gnn_b_msg.unsqueeze(0))):
                if at == OW:
                    sp.dma_start(eps1[:, :], L0_gnn_eps.partition_broadcast(P)).then_inc(s_params, 16)
                sp.dma_start(v_rows[at:at + rows.shape[0], :], rows).then_inc(s_params, 16)
            sp.wait_ge(s_setup_dve, 3)
            sp.dma_start(same_row[0:1, 0:1], zeros[0:1, 0:1].bitcast(U8)[:, 0:1]).then_inc(s_same_out, 16)
            for u in range(2):
                sp.dma_start(same_row[0, 1 + u * HALF * P:1 + (u + 1) * HALF * P].rearrange("(t e) -> t e", e=P),
                             same_rows.rearrange("p (u e) -> p u e", u=2)[0:HALF, u, :]).then_inc(s_same_out, 16)
            sp.wait_ge(s_same_out, 48)
            sp.dma_start(same[:, :], same_row[0, 0:EPAD].partition_broadcast(P)).then_inc(s_same_in, 16)
            flat = agg.rearrange("(p r) f -> p (r f)", p=P)
            for k in range(ZERO_PIECES):
                w = zeros.shape[1]
                sp.dma_start(flat[:, k * w:(k + 1) * w], zeros[:, :]).then_inc(s_zeroed, 16)
            sp.dma_start(attr_rows[0:E, :].rearrange("(a b) f -> a (b f)", b=50),
                         edge_attr_128.rearrange("(a b) f -> a (b f)", b=50)).then_inc(s_attr_copied, 16)
            sp.dma_start(attr_rows[E:EPAD, :], zeros[0:EPAD - E, 0:D]).then_inc(s_attr_copied, 16)

            def store_to(target, tail, sem_out, ready, base, rows):
                def store(c):
                    wait(sp, ready, base + c.n + 1)
                    if tail is not None and c.is_(CHUNKS - 1):
                        sp.dma_start(tail, rows[c.q][0:TAIL, :]).then_inc(sem_out[c.q], 16)
                    else:
                        sp.dma_start(target[bass.ds(c.n, 1), :, :].squeeze(0), rows[c.q]).then_inc(sem_out[c.q], 16)
                return store

            for l in range(LAYERS):
                base = CHUNKS * l
                if l:
                    for q in range(2):
                        sp.wait_ge(s_store[q], 16 * PAIRS * l)

                def load_h(c):
                    wait(sp, d_turned, base + c.n - 1)
                    if l == 0 and c.is_(CHUNKS - 1):
                        sp.dma_start(h_in[0:TAIL, c.q, :], x_tail).then_inc(s_hload[c.q], 16)
                    else:
                        rows = x_c if l == 0 else act_c
                        sp.dma_start(h_in[:, c.q, :], rows[bass.ds(c.n, 1), :, :].squeeze(0)
                                     ).then_inc(s_hload[c.q], 16)

                def load_a(c):
                    need = sp.value_load(need_row[0:1, bass.ds(c.n, 1)], min_val=0, max_val=ETILES)
                    sp.wait_ge(s_scattered, need + (ETILES * l + 1))
                    sp.dma_start(a_in[:, c.q, :], agg_c[bass.ds(c.n, 1), :, :].squeeze(0)
                                 ).then_inc(s_aload[c.q], 16)

                if l == 0:
                    sp.wait_ge(s_zeroed, 16 * ZERO_PIECES)
                    sp.wait_ge(s_setup_dve, 4)
                sweep(sp, CHUNKS, [(0, load_h), (0, load_a),
                                   (8, store_to(act_c, None, s_store, d_o, base, o_rows))])

            for q in range(2):
                sp.wait_ge(s_store[q], 16 * PAIRS * LAYERS)
            sp.wait_ge(s_gn, LAYERS)

            def load_y(c):
                wait(sp, y_turned, c.n - 1)
                sp.dma_start(h_in[:, c.q, :], act_c[bass.ds(c.n, 1), :, :].squeeze(0)).then_inc(y_hload[c.q], 16)
                wait(sp, y_z, c.n - 1)
                if c.is_(CHUNKS - 1):
                    sp.dma_start(x_in[c.q][0:TAIL, :], x_tail).then_inc(y_xload[c.q], 16)
                else:
                    sp.dma_start(x_in[c.q], x_c[bass.ds(c.n, 1), :, :].squeeze(0)).then_inc(y_xload[c.q], 16)

            sweep(sp, CHUNKS, [(0, load_y), (5, store_to(x1_c, None, y_store, y_o, 0, o_rows))])

            for q in range(2):
                sp.wait_ge(y_store[q], 16 * PAIRS)
            sp.wait_ge(s_attr_copied, 32)

            def load_attr(c):
                wait(sp, m_aT_psum, c.n - 1)
                sp.dma_start(tiles(attr_in[c.q]), attr_c[bass.ds(c.n, 1), :, :, :].squeeze(0)
                             ).then_inc(m_attr[c.q], 16)

            sweep(sp, ECHUNKS, [(0, load_attr)])
            sp.wait_ge(m_y, ECHUNKS)

            def load_f(c):
                wait(sp, f_turned, c.n - 1)
                sp.dma_start(h_in[:, c.q, :], x1_c[bass.ds(c.n, 1), :, :].squeeze(0)).then_inc(f_hload[c.q], 16)
                need = sp.value_load(need_row[0:1, bass.ds(c.n, 1)], min_val=0, max_val=ETILES)
                sp.wait_ge(s_scattered, need + (ETILES * LAYERS + 1))
                sp.dma_start(a_in[:, c.q, :], agg_c[bass.ds(c.n, 1), :, :].squeeze(0)).then_inc(f_aload[c.q], 16)

            def load_again(c):
                wait(sp, f_z, c.n - 1)
                sp.dma_start(x1_in[c.q], x1_c[bass.ds(c.n, 1), :, :].squeeze(0)).then_inc(f_xload[c.q], 16)

            sweep(sp, CHUNKS, [(0, load_f), (3, load_again), (7, store_to(out_c, out_tail, f_store, f_o, 0, out_rows))])
            for q in range(2):
                sp.wait_ge(f_store[q], 16 * PAIRS)

        @block.gpsimd
        def _(pool):
            g = nc.gpsimd
            last_row = g.to_reg(N - 1)
            g.sem_inc(s_scattered, 1)
            g.memset(idx_rows[:, 0:3 * 2 * P], NOWHERE).then_inc(s_fill, 1)
            g.memset(zeros[:, :], 0.0).then_inc(s_consts, 1)
            g.memset(v_rows, 0.0).then_inc(s_consts, 1)
            g.memset(ones[:, :], 1.0).then_inc(s_consts, 1)
            g.memset(onerow[:, :], 1.0).then_inc(s_consts, 1)
            g.memset(epsc[:, :], EPS).then_inc(s_consts, 1)
            g.memset(ident[:, :], 0.0).then_inc(s_consts, 1)
            pool.wait_ge(s_consts, 6)
            g.affine_select(out=ident[:, :], in_=ident[:, :], compare_op=ALU.not_equal, fill=1.0, base=0,
                            pattern=[[-1, P]], channel_multiplier=1).then_inc(s_consts, 1)
            g.affine_select(out=valid[:, :], in_=ones[:, 0:1], compare_op=ALU.is_gt, fill=0.0, base=TAIL,
                            pattern=[[0, 1]], channel_multiplier=-1).then_inc(s_consts, 1)
            g.iota(thr_i, pattern=[[ROWS, CHUNKS]], base=ROWS, channel_multiplier=0).then_inc(s_consts, 1)

            def run_gathers(rows, before, turned, turned_base):
                def stage(c):
                    wait(pool, turned, turned_base + c.n - 1)
                    g.sem_inc(s_tick, 1)
                    g.tensor_copy(src_now[:, c.q, :], src_tab[:, bass.ds(c.n * TILES, TILES)]).then_inc(s_src_now, 1)
                    wait(pool, s_src_now, before[0] + c.n + 1)
                    g.sem_inc(s_tick, 1)
                    for j in range(TILES):
                        g.indirect_dma_start(tile(gathered[c.q], j), None, rows,
                                             bass.IndirectOffsetOnAxis(src_now[:, c.q, j:j + 1], 0),
                                             bounds_check=last_row, oob_is_err=False).then_inc(s_gath[c.q], 16)
                sweep(pool, ECHUNKS, [(0, stage)])

            def run_scatters(phase, kept, kept_base):
                def stage(c):
                    done = EVEN[c.q] * phase + c.half
                    if not (c.fixed and c.n < 2):
                        pool.wait_ge(s_scat[c.q], 64 * done)
                        g.sem_inc(s_scattered, TILES)
                    wait(pool, kept, kept_base + c.n + 1)
                    g.sem_inc(s_tick, 1)
                    g.tensor_copy(end_now[:, c.q, :], end_tab[:, bass.ds(c.n * TILES, TILES)]).then_inc(s_end_now, 1)
                    g.tensor_copy(sum_out[:, c.q, :], sums[:, bass.ds(c.n, 1), :].squeeze(1)).then_inc(s_end_now, 1)
                    wait(pool, s_end_now, 2 * (ECHUNKS * phase + c.n + 1))
                    g.sem_inc(s_tick, 1)
                    for j in range(TILES):
                        g.indirect_dma_start(agg, bass.IndirectOffsetOnAxis(end_now[:, c.q, j:j + 1], 0),
                                             tile(sum_out[:, c.q, :], j), None,
                                             bounds_check=last_row, oob_is_err=False).then_inc(s_scat[c.q], 16)
                sweep(pool, ECHUNKS, [(0, stage)])
                for c in (ECHUNKS - 2, ECHUNKS - 1):
                    pool.wait_ge(s_scat[c % 2], 64 * (EVEN[c % 2] * phase + c // 2 + 1))
                    g.sem_inc(s_scattered, TILES)

            pool.wait_ge(s_setup_dve, 4)
            for l in range(LAYERS):
                for q in range(2):
                    wait(pool, s_store[q], 16 * PAIRS * l)
                if l:
                    pool.wait_ge(s_gn, l)
                run_gathers(x if l == 0 else act_rows, (ECHUNKS * l,), e_gT_psum, ECHUNKS * l)
                if l == 0:
                    pool.wait_ge(s_zeroed, 16 * ZERO_PIECES)
                run_scatters(l, e_y, ECHUNKS * l)
            for q in range(2):
                pool.wait_ge(y_store[q], 16 * PAIRS)
            run_gathers(x1_rows, (ECHUNKS * LAYERS,), m_gT_psum, 0)
            run_scatters(LAYERS, m_y, 0)

        @block.scalar
        def _(act):
            a = nc.scalar
            act.wait_ge(s_setup_pe, 1)
            for l in range(LAYERS):
                a.copy(linT[:, 3 * l:3 * l + 3, :].rearrange("p m f -> p (m f)"), bank[l][:, 0:3 * P]
                       ).then_inc(s_setup_act, 1)
            act.wait_ge(s_consts, 6)

            for l in range(LAYERS):
                eb, base = ECHUNKS * l, CHUNKS * l
                if l:
                    act.wait_ge(s_gn, l)

                def normed(target, source):
                    if l == 0:
                        return a.copy(target, source)
                    return a.activation(target, source, ACT.Relu, bias=gn_bias[:, l - 1:l],
                                        scale=gn_scale[:, l - 1:l])

                def edge_gT(c):
                    wait(act, e_gT_psum, eb + c.n + 1)
                    wait(act, e_scan, eb + c.n - 1)
                    normed(gT[c.q], bank[c.q][:, :]).then_inc(e_gT, 1)

                def edge_keep(c):
                    wait(act, e_yT_psum, eb + c.n + 1)
                    a.copy(sums[:, bass.ds(c.n, 1), :].squeeze(1), bank[2 + c.q][:, :]).then_inc(e_y, 1)

                sweep(act, ECHUNKS, [(0, edge_gT), (1, edge_keep)])

                def x_out(c):
                    wait(act, d_turned, base + c.n + 1)
                    wait(act, d_h0, base + c.n - 1)
                    normed(xT[c.q], b_x[:, :]).then_inc(d_xT, 1)

                def std(ready, var, sd, done, freed):
                    def stage(c):
                        wait(act, ready, base + c.n + 1)
                        wait(act, freed, base + c.n - 1)
                        a.activation(sd[:, c.q, :], var[:, c.q, :], ACT.Sqrt, bias=epsc[:, 0:1], scale=1.0 / D).then_inc(done, 1)
                    return stage

                def relu(i, turned, source, target, freed, done):
                    def stage(c):
                        wait(act, turned, base + c.n + 1)
                        wait(act, freed, base + c.n - 1)
                        a.activation(target[c.q], source[:, :], ACT.Relu, bias=col(LNB + 2 * l + i),
                                     scale=col(LNW + 2 * l + i)).then_inc(done, 1)
                    return stage

                def o_out(c):
                    wait(act, d_mm3, base + c.n + 1)
                    wait(act, s_store[c.q], 16 * (PAIRS * l + c.half))
                    wait(act, d_ost, base + c.n - 1)
                    a.copy(o_rows[c.q], b_3[:, :]).then_inc(d_o, 1)

                def norm2(c):
                    wait(act, d_r2, base + c.n + 1)
                    wait(act, d_n2T, base + c.n - 1)
                    for j in range(TILES):
                        last = a.activation(tile(n2[c.q], j), tile(b_2, j), ACT.Copy, scale=r2[:, c.q, j:j + 1])
                    last.then_inc(d_n2, 1)

                sweep(act, CHUNKS, [
                    (0, x_out), (1, std(d_var1, var1, sd1, d_sd1, d_r1)), (3, std(d_var2, var2, sd2, d_sd2, d_r2)),
                    (2, relu(0, d_n1T, b_t1, h1T, d_mm2, d_h1)), (4, relu(1, d_n2T, b_t2, h2T, d_mm3, d_h2)),
                    (5, o_out), (3, norm2)])

                act.wait_ge(s_total_pe, 2 * l + 2)
                a.activation(tot[:, 4:5], bank[0][:, 1:2], ACT.Sqrt, bias=epsc[:, 0:1],
                             scale=1.0 / (N * D)).then_inc(s_total_act, 1)

            act.wait_ge(s_gn, LAYERS)

            def y_norm(c):
                wait(act, y_turned, c.n + 1)
                wait(act, y_back, c.n - 1)
                a.activation(xT[c.q], b_x[:, :], ACT.Relu, bias=gn_bias[:, LAYERS - 1:LAYERS],
                             scale=gn_scale[:, LAYERS - 1:LAYERS]).then_inc(y_xT, 1)

            def y_std(c):
                wait(act, y_var, c.n + 1)
                wait(act, y_r, c.n - 1)
                a.activation(sd1[:, c.q, :], var1[:, c.q, :], ACT.Sqrt, bias=epsc[:, 0:1], scale=1.0 / D).then_inc(y_sd, 1)

            sweep(act, CHUNKS, [(0, y_norm), (1, y_std)])

            def m_gathered(c):
                wait(act, m_gT_psum, c.n + 1)
                wait(act, m_mm, c.n - 1)
                a.copy(gT[c.q], bank[c.q][:, :]).then_inc(m_gT, 1)

            def m_message(c):
                wait(act, m_mm, c.n + 1)
                wait(act, m_scan, c.n - 1)
                a.activation(msgT[c.q], bank[4 + c.q][:, :], ACT.Relu, bias=col(BMSG)).then_inc(m_msg, 1)

            def m_keep(c):
                wait(act, m_yT_psum, c.n + 1)
                a.copy(sums[:, bass.ds(c.n, 1), :].squeeze(1), bank[6 + c.q][:, :]).then_inc(m_y, 1)

            sweep(act, ECHUNKS, [(0, m_gathered), (1, m_message), (2, m_keep)])

            def f_xT_out(c):
                wait(act, f_turned, c.n + 1)
                wait(act, f_u, c.n - 3)
                a.copy(x1T[c.q4], b_x[:, :]).then_inc(f_xT, 1)
                wait(act, f_mm, c.n - 1)
                a.copy(meanT4[c.q], b_a[:, :]).then_inc(f_aT, 1)

            def f_std(ready, var, sd, done, freed):
                def stage(c):
                    wait(act, ready, c.n + 1)
                    wait(act, freed, c.n - 1)
                    a.activation(sd[:, c.q, :], var[:, c.q, :], ACT.Sqrt, bias=epsc[:, 0:1], scale=1.0 / D).then_inc(done, 1)
                return stage

            def f_norm(c):
                wait(act, f_r1, c.n + 1)
                wait(act, f_n1T, c.n - 1)
                for j in range(TILES):
                    last = a.activation(tile(n4[c.q], j), tile(b_1[c.q], j), ACT.Copy, scale=r1[:, c.q, j:j + 1])
                last.then_inc(f_n1, 1)

            def f_relu(c):
                wait(act, f_u, c.n + 1)
                wait(act, f_vT, c.n - 1)
                a.activation(v4[c.q], u4[c.q], ACT.Relu, bias=col(BET)).then_inc(f_v, 1)

            sweep(act, CHUNKS, [(0, f_xT_out), (1, f_std(f_var1, var1, sd1, f_sd1, f_r1)), (2, f_relu),
                                (3, f_std(f_var2, var2, sd2, f_sd2, f_r2)), (1, f_norm)], unroll=4)

        @block.vector
        def _(dve):
            v = nc.vector
            dve.wait_ge(s_idx, 16 * 9)
            for source, target in ((src_i, src_f), (dst_i, dst_f), (nxt_i, nxt_f)):
                last = v.tensor_copy(target, source)
            chain = [0]

            def step(instruction):
                chain[0] += 1
                instruction.then_inc(s_chain, 1)
                dve.wait_ge(s_chain, chain[0])

            step(last)
            step(v.tensor_tensor(end_f, dst_f, nxt_f, ALU.is_equal))
            v.tensor_copy(same_rows.rearrange("p (u e) -> p u e", u=2), end_f).then_inc(s_setup_dve, 1)
            v.scalar_tensor_tensor(out=end_f, in0=end_f, scalar=float(NOWHERE), in1=dst_f, op0=ALU.mult,
                                   op1=ALU.add).then_inc(s_setup_dve, 1)
            dve.wait_ge(s_consts, 9)
            step(v.tensor_copy(thr, thr_i))
            for u in range(2):
                last = v.tensor_scalar(reach[:, u * P:u * P + CHUNKS], thr, dst_f[:, u, 0:1], None, ALU.is_gt)
            last.then_inc(s_setup_dve, 1)
            dve.wait_ge(s_setup_pe, 2)
            for u in range(2):
                v.tensor_copy(src_tab[:, u * HALF:(u + 1) * HALF], bank[3][:, u * P:u * P + HALF])
                v.tensor_copy(end_tab[:, u * HALF:(u + 1) * HALF], bank[3][:, (2 + u) * P:(2 + u) * P + HALF])
            v.tensor_copy(need_row[0:1, :], bank[5][0:1, 0:CHUNKS])
            v.tensor_copy(cols[:, :], bank[4][:, 0:P]).then_inc(s_setup_dve, 1)
            dve.wait_ge(s_setup_act, LAYERS)
            dve.wait_ge(s_params, 16 * N_PARAMS)
            step(v.tensor_scalar(eps1[:, :], eps1[:, :], 1.0, None, ALU.add))
            step(v.reduce_sum(means9[:, 0:9], linT[:, :, :], axis=AXX))
            step(v.reduce_sum(means9[:, 9:11], w_upd[:, :, :], axis=AXX))
            step(v.reduce_sum(means9[:, 11:21], b_rows.rearrange("p (m f) -> p m f", f=D), axis=AXX))
            step(v.tensor_scalar(means9[:, 0:21], means9[:, 0:21], -1.0 / D, None, ALU.mult))
            for l in range(LAYERS):
                for i in range(2):
                    m = 3 * l + i
                    v.tensor_scalar(linT[:, m, :], linT[:, m, :], means9[:, m:m + 1], None, ALU.add)
                    last = v.tensor_scalar(b_rows[:, m * D:(m + 1) * D], b_rows[:, m * D:(m + 1) * D],
                                           means9[:, 11 + m:12 + m], None, ALU.add)
            for i in range(2):
                v.tensor_scalar(w_upd[:, i, :], w_upd[:, i, :], means9[:, 9 + i:10 + i], None, ALU.add)
            step(v.tensor_scalar(b_rows[:, 9 * D:10 * D], b_rows[:, 9 * D:10 * D], means9[:, 20:21], None, ALU.add))
            step(v.memset(pick[:, :], 0.0))
            for r in (0, 32, 64):
                v.memset(pick[r:r + 1, :], 1.0)
            step(v.memset(bias3[:, :, :], 0.0))
            flat3 = bias3[:, :, :].rearrange("p m f -> p (m f)")
            for piece in range(3):
                step(v.tensor_copy(b_bf, b_rows))
                v.tensor_copy(flat3[32 * piece:32 * piece + 32, :], b_bf[32 * piece:32 * piece + 32, :])
                step(v.tensor_copy(b_part, b_bf))
                last = v.tensor_tensor(b_rows, b_rows, b_part, ALU.subtract)
                step(last)
            v.memset(tot[:, :], 0.0).then_inc(s_setup_dve, 1)
            dve.wait_ge(s_same_in, 16)

            def layer_norm_stages(base, mm, st, s_st, var, part, s_part, s_var, sd, s_sd, r, s_r, freed, source, mean=None):
                def stats(c):
                    wait(dve, mm, base + c.n + 1)
                    for j in range(TILES):
                        last = v.bn_stats(st[:, c.q, j, :], tile(source(c), j))
                    last.then_inc(s_st, 1)

                def variance(c):
                    mean_e, m2_e, mean_o, m2_o = (st[:, c.q, :, k] for k in (1, 2, 4, 5))
                    wait(dve, s_st, base + c.n + 1)
                    v.tensor_tensor(part[:, c.q, 0, :], m2_e, m2_o, ALU.add)
                    if mean is None:
                        v.scalar_tensor_tensor(out=part[:, c.q, 1, :], in0=mean_e, scalar=float(D), in1=mean_e,
                                               op0=ALU.mult, op1=ALU.mult).then_inc(s_part, 1)
                    else:
                        v.tensor_tensor(part[:, c.q, 3, :], mean_e, mean_o, ALU.add)
                        v.tensor_tensor(part[:, c.q, 2, :], mean_e, mean_o, ALU.subtract).then_inc(s_part, 1)
                        wait(dve, s_part, 2 * (base + c.n) + 1)
                        v.tensor_scalar(mean[:, c.q, :], part[:, c.q, 3, :], 0.5, None, ALU.mult)
                        v.scalar_tensor_tensor(out=part[:, c.q, 1, :], in0=part[:, c.q, 2, :], scalar=D / 4.0,
                                               in1=part[:, c.q, 2, :], op0=ALU.mult, op1=ALU.mult).then_inc(s_part, 1)
                    wait(dve, s_part, (1 if mean is None else 2) * (base + c.n + 1))
                    v.tensor_tensor(var[:, c.q, :], part[:, c.q, 0, :], part[:, c.q, 1, :], ALU.add).then_inc(s_var, 1)

                def inverse(c):
                    wait(dve, s_sd, base + c.n + 1)
                    wait(dve, freed, base + c.n - 1)
                    v.reciprocal(r[:, c.q, :], sd[:, c.q, :]).then_inc(s_r, 1)
                return stats, variance, inverse

            for l in range(LAYERS):
                eb, base = ECHUNKS * l, CHUNKS * l

                def edge_scan(c):
                    wait(dve, e_gT, eb + c.n + 1)
                    wait(dve, e_yT_psum, eb + c.n - 1)
                    wait(dve, e_scan, eb + c.n)
                    first = 0.0 if c.is_(0) else yT[1 - c.q][:, ROWS - 1:ROWS]
                    v.tensor_tensor_scan(yT[c.q], same[:, bass.ds(c.n * ROWS, ROWS)], gT[c.q], first,
                                         ALU.mult, ALU.add).then_inc(e_scan, 1)

                sweep(dve, ECHUNKS, [(0, edge_scan)])

                def h0(c):
                    wait(dve, d_xT, base + c.n + 1)
                    wait(dve, d_mm1, base + c.n - 1)
                    v.scalar_tensor_tensor(out=h0T[c.q], in0=xT[c.q], scalar=eps1[:, l:l + 1], in1=b_a[:, :],
                                           op0=ALU.mult, op1=ALU.add).then_inc(d_h0, 1)

                stats1, variance1, inverse1 = layer_norm_stages(base, d_mm1, st1, d_st1, var1, part1, d_part1, d_var1, sd1, d_sd1, r1,
                                                           d_r1, d_n1, lambda c: b_1[c.q])
                stats2, variance2, inverse2 = layer_norm_stages(base, d_mm2, st2, d_st2, var2, part2, d_part2, d_var2, sd2, d_sd2, r2,
                                                           d_r2, d_n2, lambda c: b_2)

                def norm1(c):
                    wait(dve, d_r1, base + c.n + 1)
                    wait(dve, d_n1T, base + c.n - 1)
                    v.tensor_tensor(tiles(n1[c.q]), tiles(b_1[c.q][:, :]),
                                    r1[:, c.q, :].unsqueeze(2).to_broadcast([P, TILES, P]), ALU.mult
                                    ).then_inc(d_n1, 1)

                def out_stats(c):
                    wait(dve, d_o, base + c.n + 1)
                    v.bn_stats(st3[:, bass.ds(c.n, 1), :].squeeze(1), o_rows[c.q]).then_inc(d_ost, 1)

                sweep(dve, CHUNKS, [(1, stats1), (3, stats2), (1, variance1), (3, variance2), (0, h0), (1, inverse1),
                                    (3, inverse2), (6, out_stats), (1, norm1)])

                dve.wait_ge(d_ost, base + CHUNKS)
                step(v.tensor_scalar(st3[:, CHUNKS - 1, :], st3[:, CHUNKS - 1, :], valid[:, 0:1], None, ALU.mult))
                mean_of = st3[:, :, :].rearrange("p c (h s) -> p c h s", s=3)[:, :, :, 1]
                m2_of = st3[:, :, :].rearrange("p c (h s) -> p c h s", s=3)[:, :, :, 2]
                v.tensor_copy(dev[:, :, :], mean_of)
                step(v.tensor_reduce(out=tot[:, 1:2], in_=m2_of, axis=mybir.AxisListType.XY, op=ALU.add))
                v.tensor_reduce(out=tot[:, 0:1], in_=dev[:, :, :], axis=mybir.AxisListType.XY, op=ALU.add
                                ).then_inc(s_total_act, 1)
                dve.wait_ge(s_total_pe, 2 * l + 1)
                step(v.tensor_scalar(tot[:, 2:3], bank[0][:, 0:1], -float(STATGROUP) / (N * D), None, ALU.mult))
                step(v.tensor_scalar(dev[:, :, :], dev[:, :, :], tot[:, 2:3], None, ALU.add))
                step(v.tensor_scalar(dev[:, CHUNKS - 1, :], dev[:, CHUNKS - 1, :], valid[:, 0:1], None, ALU.mult))
                step(v.tensor_tensor(dev[:, :, :], dev[:, :, :], dev[:, :, :], ALU.mult))
                step(v.tensor_reduce(out=tot[:, 3:4], in_=dev[:, :, :], axis=mybir.AxisListType.XY, op=ALU.add))
                v.scalar_tensor_tensor(out=tot[:, 3:4], in0=tot[:, 3:4], scalar=float(STATGROUP), in1=tot[:, 1:2],
                                       op0=ALU.mult, op1=ALU.add).then_inc(s_total_act, 1)
                dve.wait_ge(s_total_act, 3 * l + 3)
                step(v.reciprocal(tot[:, 5:6], tot[:, 4:5]))
                step(v.tensor_tensor(gn_scale[:, l:l + 1], tot[:, 5:6], col(OW + l), ALU.mult))
                v.scalar_tensor_tensor(out=gn_bias[:, l:l + 1], in0=tot[:, 2:3], scalar=gn_scale[:, l:l + 1],
                                       in1=col(OB + l), op0=ALU.mult, op1=ALU.add).then_inc(s_gn, 1)

            def y_sum(c):
                wait(dve, y_back, c.n + 1)
                wait(dve, y_xload[c.q], 16 * (c.half + 1))
                wait(dve, y_o, c.n - 1)
                v.tensor_tensor(z1[c.q], b_1[c.q][:, :], x_in[c.q], ALU.add).then_inc(y_z, 1)

            y_stats, y_vars, y_inverse = layer_norm_stages(0, y_z, st1, y_st, var1, part1, y_part, y_var, sd1, y_sd, r1, y_r, y_o,
                                                           lambda c: z1[c.q], mean1)

            def y_out(c):
                wait(dve, y_r, c.n + 1)
                wait(dve, y_store[c.q], 16 * c.half)
                for j in range(TILES):
                    last = v.tensor_scalar(tile(o_rows[c.q], j), tile(z1[c.q], j), mean1[:, c.q, j:j + 1],
                                           r1[:, c.q, j:j + 1], ALU.subtract, ALU.mult)
                last.then_inc(y_o, 1)

            sweep(dve, CHUNKS, [(2, y_inverse), (1, y_sum), (2, y_out), (1, y_stats), (1, y_vars)])

            def m_attrT(c):
                wait(dve, m_aT_psum, c.n + 1)
                wait(dve, m_mm, c.n - 1)
                v.tensor_copy(attrT[c.q], bank[2 + c.q][:, :]).then_inc(m_aT, 1)

            def m_sum(c):
                mask = same[:, bass.ds(c.n * ROWS, ROWS)]
                wait(dve, m_msg, c.n + 1)
                wait(dve, m_mean, c.n)
                v.tensor_tensor_scan(count[c.q], mask, onerow[:, :],
                                     0.0 if c.is_(0) else count[1 - c.q][:, ROWS - 1:ROWS],
                                     ALU.mult, ALU.add).then_inc(m_cnt, 1)
                v.tensor_tensor_scan(yT[c.q], mask, msgT[c.q],
                                     0.0 if c.is_(0) else yT[1 - c.q][:, ROWS - 1:ROWS],
                                     ALU.mult, ALU.add).then_inc(m_scan, 1)

            def m_divide(c):
                wait(dve, m_cnt, c.n + 1)
                v.reciprocal(inv[c.q], count[c.q]).then_inc(m_inv, 1)
                wait(dve, m_inv, c.n + 1)
                wait(dve, m_scan, c.n + 1)
                wait(dve, m_yT_psum, c.n - 1)
                v.tensor_tensor(meanT[c.q], yT[c.q], inv[c.q], ALU.mult).then_inc(m_mean, 1)

            sweep(dve, ECHUNKS, [(0, m_attrT), (1, m_sum), (1, m_divide)])

            f_stats1, f_vars1, f_inverse1 = layer_norm_stages(0, f_mm, st1, f_st1, var1, part1, f_part1, f_var1, sd1, f_sd1, r1, f_r1,
                                                              f_n1, lambda c: b_1[c.q])
            f_stats2, f_vars2, f_inverse2 = layer_norm_stages(0, f_z, st2, f_st2, var2, part2, f_part2, f_var2, sd2, f_sd2, r2, f_r2,
                                                              f_o, lambda c: z4[c.q], mean2)

            def f_residual(c):
                wait(dve, f_n1T, c.n + 1)
                wait(dve, f_v, c.n - 1)
                v.scalar_tensor_tensor(out=u4[c.q], in0=b_t1[:, :], scalar=col(GAM), in1=x1T[c.q4],
                                       op0=ALU.mult, op1=ALU.add).then_inc(f_u, 1)

            def f_sum(c):
                wait(dve, f_vT, c.n + 1)
                wait(dve, f_xload[c.q], 16 * (c.half + 1))
                wait(dve, f_o, c.n - 1)
                v.tensor_tensor(z4[c.q], b_3[:, :], x1_in[c.q], ALU.add).then_inc(f_z, 1)

            def f_out(c):
                wait(dve, f_r2, c.n + 1)
                wait(dve, f_store[c.q], 16 * c.half)
                for j in range(TILES):
                    last = v.tensor_scalar(tile(out_rows[c.q], j), tile(z4[c.q], j), mean2[:, c.q, j:j + 1],
                                           r2[:, c.q, j:j + 1], ALU.subtract, ALU.mult)
                last.then_inc(f_o, 1)

            sweep(dve, CHUNKS, [(1, f_stats1), (3, f_sum), (1, f_vars1), (3, f_stats2), (4, f_inverse2), (2, f_residual),
                                (3, f_vars2), (1, f_inverse1), (4, f_out)], unroll=4)

        @block.tensor
        def _(pe):
            t = nc.tensor

            def turn(target, source):
                for j in range(TILES):
                    last = t.transpose(tile(target, j), tile(source, j), ident[:, :])
                return last

            def linear(target, hT, m, weights, more=()):
                t.matmul(tiles(target[:, :]), pick[:, :], bias3[:, m, :].unsqueeze(1).to_broadcast([P, TILES, D]),
                         start=True, stop=False)
                pairs = [(hT, weights), *more]
                for j in range(TILES):
                    for k, (lhs, w) in enumerate(pairs):
                        last = t.matmul(tile(target, j), tile(lhs, j), w, start=False,
                                        stop=(j == TILES - 1 and k == len(pairs) - 1))
                return last

            pe.wait_ge(s_consts, 9)
            pe.wait_ge(s_params, 16 * N_PARAMS)
            for m in range(9):
                last = t.transpose(bank[m // 3][:, (m % 3) * P:(m % 3 + 1) * P], w_rows[:, m * D:(m + 1) * D],
                                   ident[:, :])
            last.then_inc(s_setup_pe, 1)
            pe.wait_ge(s_setup_dve, 3)
            for u in range(2):
                t.transpose(bank[3][:, u * P:(u + 1) * P], src_f[:, u, :], ident[:, :])
                t.transpose(bank[3][:, (2 + u) * P:(3 + u) * P], end_f[:, u, :], ident[:, :])
            t.transpose(bank[4][:, 0:P], v_rows, ident[:, :])
            for u in range(2):
                last = t.matmul(bank[5][0:1, 0:CHUNKS], ones[:, 0:1], reach[:, u * P:u * P + CHUNKS],
                                start=(u == 0), stop=(u == 1))
            last.then_inc(s_setup_pe, 1)
            pe.wait_ge(s_setup_dve, 5)

            for l in range(LAYERS):
                eb, base = ECHUNKS * l, CHUNKS * l

                def edge_turn(c):
                    wait(pe, s_gath[c.q], 64 * (EVEN[c.q] * l + c.half + 1))
                    wait(pe, e_gT, eb + c.n - 1)
                    turn(bank[c.q], gathered[c.q]).then_inc(e_gT_psum, 1)

                def edge_back(c):
                    wait(pe, e_scan, eb + c.n + 1)
                    wait(pe, e_y, eb + c.n - 1)
                    turn(bank[2 + c.q], yT[c.q]).then_inc(e_yT_psum, 1)

                sweep(pe, ECHUNKS, [(0, edge_turn), (1, edge_back)])
                pe.wait_ge(e_y, eb + ECHUNKS)

                def rows_turn(c):
                    loads = 16 * (PAIRS * l + c.half + 1)
                    wait(pe, s_hload[c.q], loads)
                    wait(pe, d_xT, base + c.n)
                    turn(b_x, h_in[:, c.q, :])
                    wait(pe, s_aload[c.q], loads)
                    wait(pe, d_h0, base + c.n)
                    turn(b_a, a_in[:, c.q, :]).then_inc(d_turned, 1)

                def mm1(c):
                    wait(pe, d_h0, base + c.n + 1)
                    wait(pe, d_n1, base + c.n - 1)
                    linear(b_1[c.q], h0T[c.q], 3 * l, linT[:, 3 * l, :]).then_inc(d_mm1, 1)

                def turn1(c):
                    wait(pe, d_n1, base + c.n + 1)
                    wait(pe, d_h1, base + c.n)
                    turn(b_t1, n1[c.q]).then_inc(d_n1T, 1)

                def mm2(c):
                    wait(pe, d_h1, base + c.n + 1)
                    wait(pe, d_n2, base + c.n)
                    linear(b_2, h1T[c.q], 3 * l + 1, linT[:, 3 * l + 1, :]).then_inc(d_mm2, 1)

                def turn2(c):
                    wait(pe, d_n2, base + c.n + 1)
                    wait(pe, d_h2, base + c.n)
                    turn(b_t2, n2[c.q]).then_inc(d_n2T, 1)

                def mm3(c):
                    wait(pe, d_h2, base + c.n + 1)
                    wait(pe, d_o, base + c.n)
                    linear(b_3, h2T[c.q], 3 * l + 2, linT[:, 3 * l + 2, :]).then_inc(d_mm3, 1)

                sweep(pe, CHUNKS, [(0, rows_turn), (1, mm1), (2, turn1), (3, mm2), (4, turn2), (5, mm3)])

                for k in range(2):
                    pe.wait_ge(s_total_act, 3 * l + 1 + k)
                    t.matmul(bank[0][:, k:k + 1], ones[:, :], tot[:, 3 * k:3 * k + 1], start=True, stop=True
                             ).then_inc(s_total_pe, 1)
            pe.wait_ge(s_gn, LAYERS)

            def y_turn(c):
                wait(pe, y_hload[c.q], 16 * (c.half + 1))
                wait(pe, y_xT, c.n)
                turn(b_x, h_in[:, c.q, :]).then_inc(y_turned, 1)

            def y_turn_back(c):
                wait(pe, y_xT, c.n + 1)
                wait(pe, y_z, c.n - 1)
                turn(b_1[c.q], xT[c.q]).then_inc(y_back, 1)

            sweep(pe, CHUNKS, [(0, y_turn), (1, y_turn_back)])

            def m_turn(c):
                wait(pe, m_attr[c.q], 16 * (c.half + 1))
                wait(pe, m_aT, c.n - 1)
                turn(bank[2 + c.q], attr_in[c.q]).then_inc(m_aT_psum, 1)
                wait(pe, s_gath[c.q], 64 * (EVEN[c.q] * LAYERS + c.half + 1))
                wait(pe, m_gT, c.n - 1)
                turn(bank[c.q], gathered[c.q]).then_inc(m_gT_psum, 1)

            def m_matmul(c):
                wait(pe, m_gT, c.n + 1)
                wait(pe, m_aT, c.n + 1)
                wait(pe, m_msg, c.n - 1)
                t.matmul(bank[4 + c.q][:, :], w_msg[:, 0, :], gT[c.q], start=True, stop=False)
                t.matmul(bank[4 + c.q][:, :], w_msg[:, 1, :], attrT[c.q], start=False, stop=True).then_inc(m_mm, 1)

            def m_back(c):
                wait(pe, m_mean, c.n + 1)
                wait(pe, m_y, c.n - 1)
                turn(bank[6 + c.q], meanT[c.q]).then_inc(m_yT_psum, 1)

            pe.wait_ge(y_z, CHUNKS)
            sweep(pe, ECHUNKS, [(0, m_turn), (1, m_matmul), (2, m_back)])
            pe.wait_ge(m_y, ECHUNKS)

            def f_turn(c):
                wait(pe, f_hload[c.q], 16 * (c.half + 1))
                wait(pe, f_xT, c.n)
                turn(b_x, h_in[:, c.q, :])
                wait(pe, f_aload[c.q], 16 * (c.half + 1))
                wait(pe, f_aT, c.n)
                turn(b_a, a_in[:, c.q, :]).then_inc(f_turned, 1)

            def f_matmul(c):
                wait(pe, f_aT, c.n + 1)
                wait(pe, f_n1, c.n - 1)
                linear(b_1[c.q], x1T[c.q4], 9, w_upd[:, 0, :], [(meanT4[c.q], w_upd[:, 1, :])]).then_inc(f_mm, 1)

            def f_turn1(c):
                wait(pe, f_n1, c.n + 1)
                wait(pe, f_u, c.n)
                turn(b_t1, n4[c.q]).then_inc(f_n1T, 1)

            def f_turn2(c):
                wait(pe, f_v, c.n + 1)
                wait(pe, f_z, c.n)
                turn(b_3, v4[c.q]).then_inc(f_vT, 1)

            sweep(pe, CHUNKS, [(0, f_turn), (1, f_matmul), (2, f_turn1), (3, f_turn2)], unroll=4)


_INS = ["x", "src", "dst", "edge_attr_128", "L0_gnn_W", "L0_gnn_b", "L0_gnn_mlp_ln_w", "L0_gnn_mlp_ln_b",
        "L0_gnn_eps", "L0_gnn_out_ln_w", "L0_gnn_out_ln_b", "L1_gnn_W_msg", "L1_gnn_b_msg", "L1_gnn_W_upd",
        "L1_gnn_b_upd", "L1_gnn_gamma", "L1_gnn_beta"]


def kernel(**inputs):
    import numpy as _np
    import concourse.bacc as _bacc
    from concourse import mybir as _mybir
    from concourse.bass_utils import run_bass_kernel_spmd as _run

    nc = _bacc.Bacc("TRN2", target_bir_lowering=False, num_devices=1)
    arrays, args = {}, []
    for name in _INS:
        a = _np.ascontiguousarray(inputs[name])
        arrays[f"in_{name}"] = a
        args.append(nc.dram_tensor(f"in_{name}", a.shape, _mybir.dt.from_np(a.dtype), kind="ExternalInput").ap())
    args.append(nc.dram_tensor("out_rows_dram", (N, D), F32, kind="ExternalOutput").ap())
    build(nc, *args)
    r = _run(nc, [arrays], core_ids=[0])
    return r.results[0]["out_rows_dram"]
```

```python
from contextlib import ExitStack

import concourse.bass as bass
from concourse import mybir

F32 = mybir.dt.float32
BF16 = mybir.dt.bfloat16
I32 = mybir.dt.int32
U8 = mybir.dt.uint8
ALU = mybir.AluOpType
ACT = mybir.ActivationFunctionType
AXX = mybir.AxisListType.X

N, E, D, LAYERS = 50000, 25000, 128, 3
P = 128
TILES = 4
ROWS = P * TILES
CHUNKS = -(-N // ROWS)
NPAD = CHUNKS * ROWS
TAIL = (N - (CHUNKS - 1) * ROWS) // TILES
ECHUNKS = -(-E // ROWS)
EPAD = ECHUNKS * ROWS
ETILES = EPAD // P
HALF = ETILES // 2
FULLROWS = E // P - HALF
REST = E % P
NOWHERE = 1 << 20
EPS = 1e-5
STATGROUP = ROWS // 2
EVEN = [(ECHUNKS + 1) // 2, ECHUNKS // 2]
PAIRS = CHUNKS // 2


class Chunk:

    def __init__(self, n, half, const, fixed):
        self.n, self.half, self.q, self.q4, self.fixed = n, half, const % 2, const % 4, fixed

    def is_(self, value):
        return self.fixed and self.n == value


def sweep(eng, count, stages, unroll=2):
    deepest = max(lag for lag, _ in stages)
    lead = -(-(deepest + 2) // unroll) * unroll
    blocks = (count - 1) // unroll

    def peeled(t):
        for lag, stage in stages:
            c = t - lag
            if 0 <= c < count:
                stage(Chunk(c, c // 2, c, True))

    for t in range(lead):
        peeled(t)
    with eng.Fori(lead // unroll, blocks) as k:
        for r in range(unroll):
            for lag, stage in stages:
                const = r - lag
                stage(Chunk(k * unroll + const, k * (unroll // 2) + const // 2, const, False))
    for t in range(blocks * unroll, count + deepest):
        peeled(t)


def wait(eng, sem, value):
    if isinstance(value, int) and value <= 0:
        return
    eng.wait_ge(sem, value)


def build(nc, x, src, dst, edge_attr_128, L0_gnn_W, L0_gnn_b, L0_gnn_mlp_ln_w, L0_gnn_mlp_ln_b,
          L0_gnn_eps, L0_gnn_out_ln_w, L0_gnn_out_ln_b, L1_gnn_W_msg, L1_gnn_b_msg, L1_gnn_W_upd,
          L1_gnn_b_upd, L1_gnn_gamma, L1_gnn_beta, out):
    ctx = ExitStack()
    with ctx:
        def sb(name, shape, dt=F32):
            return ctx.enter_context(nc.sbuf_tensor(name, shape, dt))

        def sem(name):
            return ctx.enter_context(nc.semaphore(name))

        def sems(name, n=2):
            return [sem(f"{name}{i}") for i in range(n)]

        act_rows = nc.dram_tensor("act_rows", [NPAD, D], F32).ap()
        x1_rows = nc.dram_tensor("x1_rows", [NPAD, D], F32).ap()
        agg = nc.dram_tensor("agg", [NPAD, D], F32).ap()
        attr_rows = nc.dram_tensor("attr_rows", [EPAD, D], F32).ap()
        same_row = nc.dram_tensor("same_row", [1, EPAD + 1], U8).ap()

        def chunks_of(t):
            return t.rearrange("(c p j) f -> c p (j f)", p=P, j=TILES)

        act_c, x1_c, agg_c = chunks_of(act_rows), chunks_of(x1_rows), chunks_of(agg)
        WHOLE = (CHUNKS - 1) * ROWS
        x_c = chunks_of(x[0:WHOLE, :])
        x_tail = x[WHOLE:N, :].rearrange("(p j) f -> p (j f)", j=TILES)
        out_c = chunks_of(out[0:WHOLE, :])
        out_tail = out[WHOLE:N, :].rearrange("(p j) f -> p (j f)", j=TILES)
        attr_c = attr_rows.rearrange("(c j p) f -> c p j f", j=TILES, p=P)

        ident = sb("ident", [P, P])
        ones = sb("ones", [P, P])
        pick = sb("pick", [P, P], BF16)
        zeros = sb("zeros", [P, NPAD * D // P // ECHUNKS])
        onerow = sb("onerow", [P, ROWS], BF16)
        linT = sb("linT", [P, 9, D])
        w_msg = sb("w_msg", [P, 2, D])
        w_upd = sb("w_upd", [P, 2, D])
        bias3 = sb("bias3", [P, 10, D], BF16)
        cols = sb("cols", [P, P])
        eps1 = sb("eps1", [P, LAYERS])
        epsc = sb("epsc", [P, 1])
        src_tab = sb("src_tab", [P, ETILES], I32)
        end_tab = sb("end_tab", [P, ETILES], I32)
        inv_tab = sb("inv_tab", [P, ETILES])
        same = sb("same", [P, EPAD], U8)
        need_row = sb("need_row", [1, CHUNKS], I32)
        sums = sb("sums", [P, ECHUNKS, ROWS])
        h_in = sb("h_in", [P, 2, ROWS])
        a_in = sb("a_in", [P, 2, ROWS])
        work = sb("work", [P, 22, ROWS])
        sum_out = sb("sum_out", [P, 2, ROWS])
        src_now = sb("src_now", [P, 2, TILES], I32)
        end_now = sb("end_now", [P, 2, TILES], I32)
        st1 = sb("st1", [P, 2, TILES, 6])
        st2 = sb("st2", [P, 2, TILES, 6])
        var1 = sb("var1", [P, 2, TILES])
        var2 = sb("var2", [P, 2, TILES])
        part1 = sb("part1", [P, 2, 4, TILES])
        part2 = sb("part2", [P, 2, 4, TILES])
        mean1 = sb("mean1", [P, 2, TILES])
        mean2 = sb("mean2", [P, 2, TILES])
        shift = sb("shift", [P, 2, TILES])
        sd1 = sb("sd1", [P, 2, TILES])
        sd2 = sb("sd2", [P, 2, TILES])
        r1 = sb("r1", [P, 2, TILES])
        r2 = sb("r2", [P, 2, TILES])
        st3 = sb("st3", [P, CHUNKS, 6])
        dev = sb("dev", [P, CHUNKS, 2])
        valid = sb("valid", [P, 1])
        tot = sb("tot", [P, 8])
        gn_scale = sb("gn_scale", [P, LAYERS])
        gn_bias = sb("gn_bias", [P, LAYERS])

        def ring(first, n=2):
            return [work[:, first + i, :] for i in range(n)]

        xT, h0T, n1, h1T, n2, h2T, o_rows = (ring(2 * i) for i in range(7))
        gathered, gT, yT = ring(4), ring(6), ring(8)
        attr_in, attrT, msgT, count = (ring(2 * i) for i in (5, 6, 7, 8))
        x_in, z1 = ring(14), ring(16, 4)
        x1T, meanT4, n4, u4, v4, x1_in, z4, out_rows = (
            ring(0, 4), ring(4), ring(6), ring(8), ring(10), ring(12), ring(14), ring(16))

        idx_rows = work[:, 0:2, :].rearrange("p a b -> p (a b)").bitcast(I32)
        idx_f = work[:, 2:4, :].rearrange("p a b -> p (a b)")
        w_rows = work[:, 4:7, :].rearrange("p a b -> p (a b)")[:, 0:9 * D]
        b_rows = work[:, 7:10, :].rearrange("p a b -> p (a b)")[:, 0:10 * D]
        b_part = work[:, 10:13, :].rearrange("p a b -> p (a b)")[:, 0:10 * D]
        v_rows = work[:, 13, 0:P]
        thr_i = work[:, 14, 0:CHUNKS].bitcast(I32)
        thr = work[:, 14, P:P + CHUNKS]
        reach = work[:, 15, 0:2 * P]
        b_bf = work[:, 16:18, :].rearrange("p a b -> p (a b)").bitcast(BF16)[:, 0:10 * D]
        means9 = work[:, 18, 0:32]
        same_rows = work[:, 19, 0:64].bitcast(U8)

        def idx_block(t, k):
            return t[:, k * 2 * P:(k + 1) * 2 * P].rearrange("p (u e) -> p u e", u=2)

        src_i, dst_i, nxt_i = (idx_block(idx_rows, k) for k in range(3))
        src_f, dst_f, nxt_f, end_f = (idx_block(idx_f, k) for k in range(4))

        bank = [ctx.enter_context(nc.psum_tensor(f"bank{i}", [P, ROWS], F32)) for i in range(8)]
        b_x, b_a, b_t, b_3 = bank[0], bank[1], bank[2], bank[3]
        b_1, b_2 = [bank[4], bank[5]], [bank[6], bank[7]]
        b_4 = bank[4:8]

        LNW, LNB, OW, OB, GAM, BET, BMSG = 0, 6, 12, 15, 18, 19, 20

        def col(i):
            return cols[:, i:i + 1]

        def tiles(ap):
            return ap.rearrange("p (j f) -> p j f", j=TILES)

        def tile(ap, j):
            return ap[:, j * P:(j + 1) * P]

        s_consts, s_fill, s_idx, s_params, s_same_out, s_same_in = (
            sem(n) for n in ("consts", "filled", "idx_loaded", "params_loaded", "same_stored", "same_loaded"))
        s_setup_dve, s_setup_pe, s_setup_act = sem("setup_dve"), sem("setup_pe"), sem("setup_act")
        s_zeroed, s_attr_copied = sem("agg_zeroed"), sem("attr_copied")
        s_src_now, s_end_now, s_tick = sem("src_now_set"), sem("end_now_set"), sem("pool_tick")
        s_gath = sems("rows_gathered")
        s_scat = sems("rows_scattered")
        s_scattered = sem("tiles_scattered")
        e_gT_psum, e_gT, e_scan, e_yT_psum, e_y = (
            sem(n) for n in ("edge_rows_turned", "edge_gT", "edge_scanned", "edge_sums_turned", "edge_sums_kept"))
        s_hload, s_aload, s_store = sems("h_loaded"), sems("a_loaded"), sems("rows_stored")
        d_turned, d_xT, d_h0, d_mm1, d_st1, d_var1, d_sd1, d_r1, d_n1, d_n1T, d_h1 = (
            sem(n) for n in ("d_turned", "d_xT", "d_h0", "d_mm1", "d_st1", "d_var1", "d_sd1", "d_r1", "d_n1",
                             "d_n1T", "d_h1"))
        d_mm2, d_st2, d_var2, d_sd2, d_r2, d_n2, d_n2T, d_h2, d_mm3, d_o, d_ost = (
            sem(n) for n in ("d_mm2", "d_st2", "d_var2", "d_sd2", "d_r2", "d_n2", "d_n2T", "d_h2", "d_mm3", "d_o",
                             "d_ost"))
        d_part1, d_part2, y_part, f_part1, f_part2 = (sem(n) for n in ("d_part1", "d_part2", "y_part", "f_part1", "f_part2"))
        y_shift, f_shift = sem("y_shift"), sem("f_shift")
        s_chain, s_total_pe, s_total_act, s_gn = (
            sem(n) for n in ("dve_chain", "total_pe", "total_act", "graph_norm_ready"))
        y_hload, y_xload, y_store = sems("y_h_loaded"), sems("y_x_loaded"), sems("x1_stored")
        y_turned, y_xT, y_back, y_z, y_st, y_var, y_sd, y_r, y_o = (
            sem(n) for n in ("y_turned", "y_xT", "y_back", "y_z", "y_st", "y_var", "y_sd", "y_r", "y_o"))
        m_attr = sems("attr_loaded")
        m_gT_psum, m_aT_psum, m_gT, m_aT, m_mm, m_msg, m_scan, m_yT_psum, m_y = (
            sem(n) for n in ("m_gT_psum", "m_aT_psum", "m_gT", "m_aT", "m_mm", "m_msg", "m_scan", "m_yT_psum", "m_y"))
        s_count, s_count_pe, s_inv = sem("counted"), sem("counts_turned"), sem("inv_ready")
        f_hload, f_aload, f_xload, f_store = (
            sems("f_h_loaded"), sems("f_a_loaded"), sems("f_x_loaded"), sems("out_stored"))
        (f_turned, f_xT, f_aT, f_mm, f_st1, f_var1, f_sd1, f_r1, f_n1, f_n1T, f_u, f_v, f_vT, f_z, f_st2, f_var2,
         f_sd2, f_r2, f_o) = (
            sem("f_" + n) for n in ("turned", "xT", "aT", "mm", "st1", "var1", "sd1", "r1", "n1", "n1T", "u", "v",
                                    "vT", "z", "st2", "var2", "sd2", "r2", "o"))
        N_PARAMS = 13

        block = ctx.enter_context(nc.Block())

        @block.sync
        def _(sp):
            sp.wait_ge(s_fill, 1)
            for table, rows, shift in ((src, src_i, 0), (dst, dst_i, 0), (dst, nxt_i, 1)):
                first = HALF * P
                second = FULLROWS * P
                sp.dma_start(rows[0:HALF, 0, :],
                             table[shift:shift + first].rearrange("(t e) -> t e", e=P)).then_inc(s_idx, 16)
                sp.dma_start(rows[0:FULLROWS, 1, :],
                             table[shift + first:shift + first + second].rearrange("(t e) -> t e", e=P)
                             ).then_inc(s_idx, 16)
                sp.dma_start(rows[FULLROWS:FULLROWS + 1, 1, 0:REST - shift],
                             table[shift + first + second:E].unsqueeze(0)).then_inc(s_idx, 16)
            sp.wait_ge(s_consts, 6)
            sp.dma_start(w_rows.rearrange("p (m k) -> p m k", k=D),
                         L0_gnn_W.rearrange("l i o k -> o (l i) k")).then_inc(s_params, 16)
            sp.dma_start(b_rows[:, 0:9 * D],
                         L0_gnn_b.rearrange("l i o -> (l i o)").partition_broadcast(P)).then_inc(s_params, 16)
            sp.dma_start(b_rows[:, 9 * D:10 * D], L1_gnn_b_upd.partition_broadcast(P)).then_inc(s_params, 16)
            sp.dma_start(w_msg[:, :, :], L1_gnn_W_msg.rearrange("(h k) f -> k h f", k=P)).then_inc(s_params, 16)
            sp.dma_start(w_upd[:, :, :], L1_gnn_W_upd.rearrange("(h k) f -> k h f", k=P)).then_inc(s_params, 16)
            for at, rows in ((LNW, L0_gnn_mlp_ln_w.rearrange("l i f -> (l i) f")),
                             (LNB, L0_gnn_mlp_ln_b.rearrange("l i f -> (l i) f")),
                             (OW, L0_gnn_out_ln_w), (OB, L0_gnn_out_ln_b), (GAM, L1_gnn_gamma.unsqueeze(0)),
                             (BET, L1_gnn_beta.unsqueeze(0)), (BMSG, L1_gnn_b_msg.unsqueeze(0))):
                if at == OW:
                    sp.dma_start(eps1[:, :], L0_gnn_eps.partition_broadcast(P)).then_inc(s_params, 16)
                sp.dma_start(v_rows[at:at + rows.shape[0], :], rows).then_inc(s_params, 16)
            sp.wait_ge(s_setup_dve, 3)
            sp.dma_start(same_row[0:1, 0:1], zeros[0:1, 0:1].bitcast(U8)[:, 0:1]).then_inc(s_same_out, 16)
            for u in range(2):
                sp.dma_start(same_row[0, 1 + u * HALF * P:1 + (u + 1) * HALF * P].rearrange("(t e) -> t e", e=P),
                             same_rows.rearrange("p (u e) -> p u e", u=2)[0:HALF, u, :]).then_inc(s_same_out, 16)
            sp.wait_ge(s_same_out, 48)
            sp.dma_start(same[:, :], same_row[0, 0:EPAD].partition_broadcast(P)).then_inc(s_same_in, 16)
            flat = agg.rearrange("(p k r) f -> k p (r f)", p=P, k=ECHUNKS)

            def zero_piece(c):
                wait(sp, e_gT_psum, c.n)
                sp.dma_start(flat[bass.ds(c.n, 1), :, :].squeeze(0), zeros[:, :]).then_inc(s_zeroed, 16)

            sweep(sp, ECHUNKS, [(0, zero_piece)])

            def store_to(target, tail, sem_out, ready, base, rows):
                def store(c):
                    wait(sp, ready, base + c.n + 1)
                    if tail is not None and c.is_(CHUNKS - 1):
                        sp.dma_start(tail, rows[c.q][0:TAIL, :]).then_inc(sem_out[c.q], 16)
                    else:
                        sp.dma_start(target[bass.ds(c.n, 1), :, :].squeeze(0), rows[c.q]).then_inc(sem_out[c.q], 16)
                return store

            for l in range(LAYERS):
                base = CHUNKS * l
                if l:
                    for q in range(2):
                        sp.wait_ge(s_store[q], 16 * PAIRS * l)

                if l == 1:
                    attr_out = attr_rows.rearrange("(c p j) f -> c p (j f)", p=P, j=TILES)
                    attr_from = edge_attr_128[0:(ECHUNKS - 1) * ROWS, :].rearrange(
                        "(c p j) f -> c p (j f)", p=P, j=TILES)

                    def attr_piece(c):
                        wait(sp, e_gT_psum, ECHUNKS + c.n)
                        sp.dma_start(attr_out[bass.ds(c.n, 1), :, :].squeeze(0),
                                     attr_from[bass.ds(c.n, 1), :, :].squeeze(0)).then_inc(s_attr_copied, 16)

                    sweep(sp, ECHUNKS - 1, [(0, attr_piece)])
                    sp.dma_start(attr_rows[(ECHUNKS - 1) * ROWS:E, :], edge_attr_128[(ECHUNKS - 1) * ROWS:E, :]
                                 ).then_inc(s_attr_copied, 16)
                    sp.dma_start(attr_rows[E:EPAD, :], zeros[0:EPAD - E, 0:D]).then_inc(s_attr_copied, 16)

                def load_h(c):
                    wait(sp, d_turned, base + c.n - 1)
                    if l == 0 and c.is_(CHUNKS - 1):
                        sp.dma_start(h_in[0:TAIL, c.q, :], x_tail).then_inc(s_hload[c.q], 16)
                    else:
                        rows = x_c if l == 0 else act_c
                        sp.dma_start(h_in[:, c.q, :], rows[bass.ds(c.n, 1), :, :].squeeze(0)
                                     ).then_inc(s_hload[c.q], 16)

                def load_a(c):
                    need = sp.value_load(need_row[0:1, bass.ds(c.n, 1)], min_val=0, max_val=ETILES)
                    sp.wait_ge(s_scattered, need + (ETILES * l + 1))
                    sp.dma_start(a_in[:, c.q, :], agg_c[bass.ds(c.n, 1), :, :].squeeze(0)
                                 ).then_inc(s_aload[c.q], 16)

                if l == 0:
                    sp.wait_ge(s_zeroed, 16 * ECHUNKS)
                    sp.wait_ge(s_setup_dve, 4)
                sweep(sp, CHUNKS, [(0, load_h), (0, load_a),
                                   (9, store_to(act_c, None, s_store, d_o, base, o_rows))])

            for q in range(2):
                sp.wait_ge(s_store[q], 16 * PAIRS * LAYERS)
            sp.wait_ge(s_gn, LAYERS)

            def load_y(c):
                wait(sp, y_turned, c.n - 1)
                sp.dma_start(h_in[:, c.q, :], act_c[bass.ds(c.n, 1), :, :].squeeze(0)).then_inc(y_hload[c.q], 16)
                wait(sp, y_z, c.n - 1)
                if c.is_(CHUNKS - 1):
                    sp.dma_start(x_in[c.q][0:TAIL, :], x_tail).then_inc(y_xload[c.q], 16)
                else:
                    sp.dma_start(x_in[c.q], x_c[bass.ds(c.n, 1), :, :].squeeze(0)).then_inc(y_xload[c.q], 16)

            sweep(sp, CHUNKS, [(0, load_y), (5, store_to(x1_c, None, y_store, y_o, 0, o_rows))])

            for q in range(2):
                sp.wait_ge(y_store[q], 16 * PAIRS)
            sp.wait_ge(s_attr_copied, 16 * (ECHUNKS + 1))

            def load_attr(c):
                wait(sp, m_aT_psum, c.n - 1)
                sp.dma_start(tiles(attr_in[c.q]), attr_c[bass.ds(c.n, 1), :, :, :].squeeze(0)
                             ).then_inc(m_attr[c.q], 16)

            sweep(sp, ECHUNKS, [(0, load_attr)])
            sp.wait_ge(m_y, ECHUNKS)

            def load_f(c):
                wait(sp, f_turned, c.n - 1)
                sp.dma_start(h_in[:, c.q, :], x1_c[bass.ds(c.n, 1), :, :].squeeze(0)).then_inc(f_hload[c.q], 16)
                need = sp.value_load(need_row[0:1, bass.ds(c.n, 1)], min_val=0, max_val=ETILES)
                sp.wait_ge(s_scattered, need + (ETILES * LAYERS + 1))
                sp.dma_start(a_in[:, c.q, :], agg_c[bass.ds(c.n, 1), :, :].squeeze(0)).then_inc(f_aload[c.q], 16)

            def load_again(c):
                wait(sp, f_z, c.n - 1)
                sp.dma_start(x1_in[c.q], x1_c[bass.ds(c.n, 1), :, :].squeeze(0)).then_inc(f_xload[c.q], 16)

            sweep(sp, CHUNKS, [(0, load_f), (5, load_again), (8, store_to(out_c, out_tail, f_store, f_o, 0, out_rows))])
            for q in range(2):
                sp.wait_ge(f_store[q], 16 * PAIRS)

        @block.gpsimd
        def _(pool):
            g = nc.gpsimd
            last_row = g.to_reg(N - 1)
            g.sem_inc(s_scattered, 1)
            g.memset(idx_rows[:, 0:3 * 2 * P], NOWHERE).then_inc(s_fill, 1)
            g.memset(zeros[:, :], 0.0).then_inc(s_consts, 1)
            g.memset(v_rows, 0.0).then_inc(s_consts, 1)
            g.memset(ones[:, :], 1.0).then_inc(s_consts, 1)
            g.memset(onerow[:, :], 1.0).then_inc(s_consts, 1)
            g.memset(epsc[:, :], EPS).then_inc(s_consts, 1)
            g.memset(ident[:, :], 0.0).then_inc(s_consts, 1)
            pool.wait_ge(s_consts, 6)
            g.affine_select(out=ident[:, :], in_=ident[:, :], compare_op=ALU.not_equal, fill=1.0, base=0,
                            pattern=[[-1, P]], channel_multiplier=1).then_inc(s_consts, 1)
            g.affine_select(out=valid[:, :], in_=ones[:, 0:1], compare_op=ALU.is_gt, fill=0.0, base=TAIL,
                            pattern=[[0, 1]], channel_multiplier=-1).then_inc(s_consts, 1)
            g.iota(thr_i, pattern=[[ROWS, CHUNKS]], base=ROWS, channel_multiplier=0).then_inc(s_consts, 1)

            def run_gathers(rows, phase):
                def stage(c):
                    wait(pool, s_src_now, ECHUNKS * phase + c.n + 1)
                    g.sem_inc(s_tick, 1)
                    for j in range(TILES):
                        g.indirect_dma_start(tile(gathered[c.q], j), None, rows,
                                             bass.IndirectOffsetOnAxis(src_now[:, c.q, j:j + 1], 0),
                                             bounds_check=last_row, oob_is_err=False).then_inc(s_gath[c.q], 16)
                sweep(pool, ECHUNKS, [(0, stage)])

            def run_scatters(phase, kept, kept_base):
                def stage(c):
                    done = EVEN[c.q] * phase + c.half
                    if not (c.fixed and c.n < 2):
                        pool.wait_ge(s_scat[c.q], 64 * done)
                        g.sem_inc(s_scattered, TILES)
                    wait(pool, kept, kept_base + c.n + 1)
                    g.sem_inc(s_tick, 1)
                    g.tensor_copy(end_now[:, c.q, :], end_tab[:, bass.ds(c.n * TILES, TILES)]).then_inc(s_end_now, 1)
                    g.tensor_copy(sum_out[:, c.q, :], sums[:, bass.ds(c.n, 1), :].squeeze(1)).then_inc(s_end_now, 1)
                    wait(pool, s_end_now, 2 * (ECHUNKS * phase + c.n + 1))
                    g.sem_inc(s_tick, 1)
                    for j in range(TILES):
                        g.indirect_dma_start(agg, bass.IndirectOffsetOnAxis(end_now[:, c.q, j:j + 1], 0),
                                             tile(sum_out[:, c.q, :], j), None,
                                             bounds_check=last_row, oob_is_err=False).then_inc(s_scat[c.q], 16)
                sweep(pool, ECHUNKS, [(0, stage)])
                for c in (ECHUNKS - 2, ECHUNKS - 1):
                    pool.wait_ge(s_scat[c % 2], 64 * (EVEN[c % 2] * phase + c // 2 + 1))
                    g.sem_inc(s_scattered, TILES)

            pool.wait_ge(s_setup_dve, 4)
            for l in range(LAYERS):
                for q in range(2):
                    wait(pool, s_store[q], 16 * PAIRS * l)
                if l:
                    pool.wait_ge(s_gn, l)
                run_gathers(x if l == 0 else act_rows, l)
                if l == 0:
                    pool.wait_ge(s_zeroed, 16 * ECHUNKS)
                run_scatters(l, e_y, ECHUNKS * l)
            for q in range(2):
                pool.wait_ge(y_store[q], 16 * PAIRS)
            run_gathers(x1_rows, LAYERS)
            run_scatters(LAYERS, m_y, 0)

        @block.scalar
        def _(act):
            a = nc.scalar
            act.wait_ge(s_setup_pe, 1)
            for l in range(LAYERS):
                a.copy(linT[:, 3 * l:3 * l + 3, :].rearrange("p m f -> p (m f)"), bank[l][:, 0:3 * P]
                       ).then_inc(s_setup_act, 1)
            act.wait_ge(s_consts, 6)

            for l in range(LAYERS):
                eb, base = ECHUNKS * l, CHUNKS * l
                if l:
                    act.wait_ge(s_gn, l)

                def normed(target, source):
                    if l == 0:
                        return a.copy(target, source)
                    return a.activation(target, source, ACT.Relu, bias=gn_bias[:, l - 1:l],
                                        scale=gn_scale[:, l - 1:l])

                def edge_gT(c):
                    wait(act, e_gT_psum, eb + c.n + 1)
                    wait(act, e_scan, eb + c.n - 1)
                    normed(gT[c.q], bank[c.q][:, :]).then_inc(e_gT, 1)

                def edge_keep(c):
                    wait(act, e_yT_psum, eb + c.n + 1)
                    a.copy(sums[:, bass.ds(c.n, 1), :].squeeze(1), bank[2 + c.q][:, :]).then_inc(e_y, 1)

                sweep(act, ECHUNKS, [(0, edge_gT), (1, edge_keep)])

                def x_out(c):
                    wait(act, d_turned, base + c.n + 1)
                    wait(act, d_h0, base + c.n - 1)
                    normed(xT[c.q], b_x[:, :]).then_inc(d_xT, 1)

                def std(ready, var, sd, done, freed):
                    def stage(c):
                        wait(act, ready, base + c.n + 1)
                        wait(act, freed, base + c.n - 1)
                        a.activation(sd[:, c.q, :], var[:, c.q, :], ACT.Sqrt, bias=epsc[:, 0:1], scale=1.0 / D).then_inc(done, 1)
                    return stage

                def relu(i, turned, target, freed, done):
                    def stage(c):
                        wait(act, turned, base + c.n + 1)
                        wait(act, freed, base + c.n - 1)
                        a.activation(target[c.q], b_t[:, :], ACT.Relu, bias=col(LNB + 2 * l + i),
                                     scale=col(LNW + 2 * l + i)).then_inc(done, 1)
                    return stage

                def o_out(c):
                    wait(act, d_mm3, base + c.n + 1)
                    wait(act, s_store[c.q], 16 * (PAIRS * l + c.half))
                    wait(act, d_ost, base + c.n - 1)
                    a.copy(o_rows[c.q], b_3[:, :]).then_inc(d_o, 1)

                def norm2(c):
                    wait(act, d_r2, base + c.n + 1)
                    wait(act, d_n2T, base + c.n - 1)
                    for j in range(TILES):
                        last = a.activation(tile(n2[c.q], j), tile(b_2[c.q], j), ACT.Copy, scale=r2[:, c.q, j:j + 1])
                    last.then_inc(d_n2, 1)

                sweep(act, CHUNKS, [
                    (0, x_out), (4, std(d_var2, var2, sd2, d_sd2, d_r2)), (2, relu(0, d_n1T, h1T, d_mm2, d_h1)),
                    (4, norm2), (1, std(d_var1, var1, sd1, d_sd1, d_r1)), (5, relu(1, d_n2T, h2T, d_mm3, d_h2)),
                    (6, o_out)])

                act.wait_ge(s_total_pe, 2 * l + 2)
                a.activation(tot[:, 4:5], bank[0][:, 1:2], ACT.Sqrt, bias=epsc[:, 0:1],
                             scale=1.0 / (N * D)).then_inc(s_total_act, 1)

            act.wait_ge(s_gn, LAYERS)
            act.wait_ge(s_inv, 1)

            def y_norm(c):
                wait(act, y_turned, c.n + 1)
                wait(act, y_back, c.n - 1)
                a.activation(xT[c.q], b_x[:, :], ACT.Relu, bias=gn_bias[:, LAYERS - 1:LAYERS],
                             scale=gn_scale[:, LAYERS - 1:LAYERS]).then_inc(y_xT, 1)

            def y_std(c):
                wait(act, y_var, c.n + 1)
                wait(act, y_r, c.n - 1)
                a.activation(sd1[:, c.q, :], var1[:, c.q, :], ACT.Sqrt, bias=epsc[:, 0:1], scale=1.0 / D).then_inc(y_sd, 1)

            def scaled_rows(c, target, source, r, done):
                for j in range(TILES):
                    last = a.activation(tile(target[c.q], j), tile(source, j), ACT.Identity,
                                        bias=shift[:, c.q, j:j + 1], scale=r[:, c.q, j:j + 1])
                last.then_inc(done, 1)

            def y_out(c):
                wait(act, y_shift, c.n + 1)
                wait(act, y_store[c.q], 16 * c.half)
                scaled_rows(c, o_rows, z1[c.q4], r1, y_o)

            sweep(act, CHUNKS, [(3, y_std), (0, y_norm), (4, y_out)], unroll=4)

            def m_gathered(c):
                wait(act, m_gT_psum, c.n + 1)
                wait(act, m_mm, c.n - 1)
                a.copy(gT[c.q], bank[c.q][:, :]).then_inc(m_gT, 1)

            def m_message(c):
                wait(act, m_mm, c.n + 1)
                wait(act, m_scan, c.n - 1)
                a.activation(msgT[c.q], bank[4 + c.q][:, :], ACT.Relu, bias=col(BMSG)).then_inc(m_msg, 1)

            def m_keep(c):
                wait(act, m_yT_psum, c.n + 1)
                for j in range(TILES):
                    last = a.activation(sums[:, bass.ds(c.n, 1), j * P:(j + 1) * P].squeeze(1), tile(bank[6 + c.q], j),
                                        ACT.Copy, scale=inv_tab[:, bass.ds(c.n * TILES + j, 1)])
                last.then_inc(m_y, 1)

            sweep(act, ECHUNKS, [(0, m_gathered), (1, m_message), (2, m_keep)])

            def f_xT_out(c):
                wait(act, f_turned, c.n + 1)
                wait(act, f_u, c.n - 3)
                a.copy(x1T[c.q4], b_x[:, :]).then_inc(f_xT, 1)
                wait(act, f_mm, c.n - 1)
                a.copy(meanT4[c.q], b_a[:, :]).then_inc(f_aT, 1)

            def f_std(ready, var, sd, done, freed):
                def stage(c):
                    wait(act, ready, c.n + 1)
                    wait(act, freed, c.n - 1)
                    a.activation(sd[:, c.q, :], var[:, c.q, :], ACT.Sqrt, bias=epsc[:, 0:1], scale=1.0 / D).then_inc(done, 1)
                return stage

            def f_norm(c):
                wait(act, f_r1, c.n + 1)
                wait(act, f_n1T, c.n - 1)
                for j in range(TILES):
                    last = a.activation(tile(n4[c.q], j), tile(b_4[c.q4], j), ACT.Copy, scale=r1[:, c.q, j:j + 1])
                last.then_inc(f_n1, 1)

            def f_relu(c):
                wait(act, f_u, c.n + 1)
                wait(act, f_vT, c.n - 1)
                a.activation(v4[c.q], u4[c.q], ACT.Relu, bias=col(BET)).then_inc(f_v, 1)

            def f_out(c):
                wait(act, f_shift, c.n + 1)
                wait(act, f_store[c.q], 16 * c.half)
                scaled_rows(c, out_rows, z4[c.q], r2, f_o)

            sweep(act, CHUNKS, [(2, f_std(f_var1, var1, sd1, f_sd1, f_r1)), (5, f_std(f_var2, var2, sd2, f_sd2, f_r2)),
                                (0, f_xT_out), (3, f_relu), (2, f_norm), (5, f_out)], unroll=4)

        @block.vector
        def _(dve):
            v = nc.vector
            dve.wait_ge(s_idx, 16 * 9)
            for source, target in ((src_i, src_f), (dst_i, dst_f), (nxt_i, nxt_f)):
                last = v.tensor_copy(target, source)
            chain = [0]

            def step(instruction):
                chain[0] += 1
                instruction.then_inc(s_chain, 1)
                dve.wait_ge(s_chain, chain[0])

            step(last)
            step(v.tensor_tensor(end_f, dst_f, nxt_f, ALU.is_equal))
            v.tensor_copy(same_rows.rearrange("p (u e) -> p u e", u=2), end_f).then_inc(s_setup_dve, 1)
            v.scalar_tensor_tensor(out=end_f, in0=end_f, scalar=float(NOWHERE), in1=dst_f, op0=ALU.mult,
                                   op1=ALU.add).then_inc(s_setup_dve, 1)
            dve.wait_ge(s_consts, 9)
            step(v.tensor_copy(thr, thr_i))
            for u in range(2):
                last = v.tensor_scalar(reach[:, u * P:u * P + CHUNKS], thr, dst_f[:, u, 0:1], None, ALU.is_gt)
            last.then_inc(s_setup_dve, 1)
            dve.wait_ge(s_setup_pe, 2)
            for u in range(2):
                v.tensor_copy(src_tab[:, u * HALF:(u + 1) * HALF], bank[3][:, u * P:u * P + HALF])
                v.tensor_copy(end_tab[:, u * HALF:(u + 1) * HALF], bank[3][:, (2 + u) * P:(2 + u) * P + HALF])
            v.tensor_copy(need_row[0:1, :], bank[5][0:1, 0:CHUNKS])
            v.tensor_copy(cols[:, :], bank[4][:, 0:P]).then_inc(s_setup_dve, 1)
            dve.wait_ge(s_setup_act, LAYERS)
            dve.wait_ge(s_params, 16 * N_PARAMS)
            step(v.tensor_scalar(eps1[:, :], eps1[:, :], 1.0, None, ALU.add))
            step(v.reduce_sum(means9[:, 0:9], linT[:, :, :], axis=AXX))
            step(v.reduce_sum(means9[:, 9:11], w_upd[:, :, :], axis=AXX))
            step(v.reduce_sum(means9[:, 11:21], b_rows.rearrange("p (m f) -> p m f", f=D), axis=AXX))
            step(v.tensor_scalar(means9[:, 0:21], means9[:, 0:21], -1.0 / D, None, ALU.mult))
            for l in range(LAYERS):
                for i in range(2):
                    m = 3 * l + i
                    v.tensor_scalar(linT[:, m, :], linT[:, m, :], means9[:, m:m + 1], None, ALU.add)
                    last = v.tensor_scalar(b_rows[:, m * D:(m + 1) * D], b_rows[:, m * D:(m + 1) * D],
                                           means9[:, 11 + m:12 + m], None, ALU.add)
            for i in range(2):
                v.tensor_scalar(w_upd[:, i, :], w_upd[:, i, :], means9[:, 9 + i:10 + i], None, ALU.add)
            step(v.tensor_scalar(b_rows[:, 9 * D:10 * D], b_rows[:, 9 * D:10 * D], means9[:, 20:21], None, ALU.add))
            step(v.memset(pick[:, :], 0.0))
            for r in (0, 32, 64):
                v.memset(pick[r:r + 1, :], 1.0)
            step(v.memset(bias3[:, :, :], 0.0))
            flat3 = bias3[:, :, :].rearrange("p m f -> p (m f)")
            for piece in range(3):
                step(v.tensor_copy(b_bf, b_rows))
                v.tensor_copy(flat3[32 * piece:32 * piece + 32, :], b_bf[32 * piece:32 * piece + 32, :])
                step(v.tensor_copy(b_part, b_bf))
                last = v.tensor_tensor(b_rows, b_rows, b_part, ALU.subtract)
                step(last)
            v.memset(tot[:, :], 0.0).then_inc(s_setup_dve, 1)
            dve.wait_ge(s_same_in, 16)

            def layer_norm_stages(base, mm, st, s_st, var, part, s_part, s_var, sd, s_sd, r, s_r, freed, source, mean=None):
                def stats(c):
                    wait(dve, mm, base + c.n + 1)
                    for j in range(TILES):
                        last = v.bn_stats(st[:, c.q, j, :], tile(source(c), j))
                    last.then_inc(s_st, 1)

                def variance(c):
                    mean_e, m2_e, mean_o, m2_o = (st[:, c.q, :, k] for k in (1, 2, 4, 5))
                    wait(dve, s_st, base + c.n + 1)
                    v.tensor_tensor(part[:, c.q, 0, :], m2_e, m2_o, ALU.add)
                    if mean is None:
                        v.scalar_tensor_tensor(out=part[:, c.q, 1, :], in0=mean_e, scalar=float(D), in1=mean_e,
                                               op0=ALU.mult, op1=ALU.mult).then_inc(s_part, 1)
                    else:
                        v.tensor_tensor(part[:, c.q, 3, :], mean_e, mean_o, ALU.add)
                        v.tensor_tensor(part[:, c.q, 2, :], mean_e, mean_o, ALU.subtract).then_inc(s_part, 1)
                        wait(dve, s_part, 2 * (base + c.n) + 1)
                        v.tensor_scalar(mean[:, c.q, :], part[:, c.q, 3, :], 0.5, None, ALU.mult)
                        v.scalar_tensor_tensor(out=part[:, c.q, 1, :], in0=part[:, c.q, 2, :], scalar=D / 4.0,
                                               in1=part[:, c.q, 2, :], op0=ALU.mult, op1=ALU.mult).then_inc(s_part, 1)
                    wait(dve, s_part, (1 if mean is None else 2) * (base + c.n + 1))
                    v.tensor_tensor(var[:, c.q, :], part[:, c.q, 0, :], part[:, c.q, 1, :], ALU.add).then_inc(s_var, 1)

                def inverse(c):
                    wait(dve, s_sd, base + c.n + 1)
                    wait(dve, freed, base + c.n - 1)
                    v.reciprocal(r[:, c.q, :], sd[:, c.q, :]).then_inc(s_r, 1)
                return stats, variance, inverse

            def next_sources(turned, base):
                def stage(c):
                    wait(dve, turned, base + c.n - 1)
                    v.tensor_copy(src_now[:, c.q, :], src_tab[:, bass.ds(c.n * TILES, TILES)]).then_inc(s_src_now, 1)
                return stage

            def run_sum(ready, freed, done, base, source):
                def stage(c):
                    wait(dve, ready, base + c.n + 1)
                    wait(dve, freed, base + c.n - 1)
                    wait(dve, done, base + c.n)
                    first = 0.0 if c.is_(0) else yT[1 - c.q][:, ROWS - 1:ROWS]
                    v.tensor_tensor_scan(yT[c.q], same[:, bass.ds(c.n * ROWS, ROWS)], source[c.q], first,
                                         ALU.mult, ALU.add).then_inc(done, 1)
                return stage

            for l in range(LAYERS):
                eb, base = ECHUNKS * l, CHUNKS * l

                stages = [(0, next_sources(e_gT_psum, eb)), (2, run_sum(e_gT, e_yT_psum, e_scan, eb, gT))]
                if l == 0:
                    def edge_count(c):
                        wait(dve, s_count, c.n)
                        wait(dve, s_count_pe, c.n - 1)
                        first = 0.0 if c.is_(0) else count[1 - c.q][0:1, ROWS - 1:ROWS]
                        v.tensor_tensor_scan(count[c.q][0:1, :], same[0:1, bass.ds(c.n * ROWS, ROWS)], onerow[0:1, :],
                                             first, ALU.mult, ALU.add).then_inc(s_count, 1)
                    stages.append((2, edge_count))
                sweep(dve, ECHUNKS, stages)
                if l == 0:
                    dve.wait_ge(s_count_pe, ECHUNKS)
                    v.reciprocal(inv_tab[:, :], bank[4][:, 0:ETILES]).then_inc(s_inv, 1)

                def h0(c):
                    wait(dve, d_xT, base + c.n + 1)
                    wait(dve, d_mm1, base + c.n - 1)
                    v.scalar_tensor_tensor(out=h0T[c.q], in0=xT[c.q], scalar=eps1[:, l:l + 1], in1=b_a[:, :],
                                           op0=ALU.mult, op1=ALU.add).then_inc(d_h0, 1)

                stats1, variance1, inverse1 = layer_norm_stages(base, d_mm1, st1, d_st1, var1, part1, d_part1, d_var1, sd1, d_sd1, r1,
                                                           d_r1, d_n1, lambda c: b_1[c.q])
                stats2, variance2, inverse2 = layer_norm_stages(base, d_mm2, st2, d_st2, var2, part2, d_part2, d_var2, sd2, d_sd2, r2,
                                                           d_r2, d_n2, lambda c: b_2[c.q])

                def norm1(c):
                    wait(dve, d_r1, base + c.n + 1)
                    wait(dve, d_n1T, base + c.n - 1)
                    v.tensor_tensor(tiles(n1[c.q]), tiles(b_1[c.q][:, :]),
                                    r1[:, c.q, :].unsqueeze(2).to_broadcast([P, TILES, P]), ALU.mult
                                    ).then_inc(d_n1, 1)

                def out_stats(c):
                    wait(dve, d_o, base + c.n + 1)
                    v.bn_stats(st3[:, bass.ds(c.n, 1), :].squeeze(1), o_rows[c.q]).then_inc(d_ost, 1)

                sweep(dve, CHUNKS, [(4, stats2), (4, variance2), (0, h0), (4, inverse2), (1, stats1), (1, variance1),
                                    (7, out_stats), (1, inverse1), (1, norm1)])

                dve.wait_ge(d_ost, base + CHUNKS)
                step(v.tensor_scalar(st3[:, CHUNKS - 1, :], st3[:, CHUNKS - 1, :], valid[:, 0:1], None, ALU.mult))
                mean_of = st3[:, :, :].rearrange("p c (h s) -> p c h s", s=3)[:, :, :, 1]
                m2_of = st3[:, :, :].rearrange("p c (h s) -> p c h s", s=3)[:, :, :, 2]
                v.tensor_copy(dev[:, :, :], mean_of)
                step(v.tensor_reduce(out=tot[:, 1:2], in_=m2_of, axis=mybir.AxisListType.XY, op=ALU.add))
                v.tensor_reduce(out=tot[:, 0:1], in_=dev[:, :, :], axis=mybir.AxisListType.XY, op=ALU.add
                                ).then_inc(s_total_act, 1)
                dve.wait_ge(s_total_pe, 2 * l + 1)
                step(v.tensor_scalar(tot[:, 2:3], bank[0][:, 0:1], -float(STATGROUP) / (N * D), None, ALU.mult))
                step(v.tensor_scalar(dev[:, :, :], dev[:, :, :], tot[:, 2:3], None, ALU.add))
                step(v.tensor_scalar(dev[:, CHUNKS - 1, :], dev[:, CHUNKS - 1, :], valid[:, 0:1], None, ALU.mult))
                step(v.tensor_tensor(dev[:, :, :], dev[:, :, :], dev[:, :, :], ALU.mult))
                step(v.tensor_reduce(out=tot[:, 3:4], in_=dev[:, :, :], axis=mybir.AxisListType.XY, op=ALU.add))
                v.scalar_tensor_tensor(out=tot[:, 3:4], in0=tot[:, 3:4], scalar=float(STATGROUP), in1=tot[:, 1:2],
                                       op0=ALU.mult, op1=ALU.add).then_inc(s_total_act, 1)
                dve.wait_ge(s_total_act, 3 * l + 3)
                step(v.reciprocal(tot[:, 5:6], tot[:, 4:5]))
                step(v.tensor_tensor(gn_scale[:, l:l + 1], tot[:, 5:6], col(OW + l), ALU.mult))
                v.scalar_tensor_tensor(out=gn_bias[:, l:l + 1], in0=tot[:, 2:3], scalar=gn_scale[:, l:l + 1],
                                       in1=col(OB + l), op0=ALU.mult, op1=ALU.add).then_inc(s_gn, 1)

            def y_sum(c):
                wait(dve, y_back, c.n + 1)
                wait(dve, y_xload[c.q], 16 * (c.half + 1))
                wait(dve, y_o, c.n - 3)
                v.tensor_tensor(z1[c.q4], b_1[c.q][:, :], x_in[c.q], ALU.add).then_inc(y_z, 1)

            y_stats, y_vars, y_inverse = layer_norm_stages(0, y_z, st1, y_st, var1, part1, y_part, y_var, sd1, y_sd, r1, y_r, y_o,
                                                           lambda c: z1[c.q4], mean1)

            def shift_stage(mean, r, s_r, done):
                def stage(c):
                    wait(dve, s_r, c.n + 1)
                    v.scalar_tensor_tensor(out=shift[:, c.q, :], in0=mean[:, c.q, :], scalar=-1.0, in1=r[:, c.q, :],
                                           op0=ALU.mult, op1=ALU.mult).then_inc(done, 1)
                return stage

            sweep(dve, CHUNKS, [(3, y_inverse), (2, y_sum), (3, shift_stage(mean1, r1, y_r, y_shift)), (2, y_stats),
                                (2, y_vars)], unroll=4)

            def m_attrT(c):
                wait(dve, m_aT_psum, c.n + 1)
                wait(dve, m_mm, c.n - 1)
                v.tensor_copy(attrT[c.q], bank[2 + c.q][:, :]).then_inc(m_aT, 1)

            sweep(dve, ECHUNKS, [(0, next_sources(m_gT_psum, 0)), (1, m_attrT),
                                 (3, run_sum(m_msg, m_yT_psum, m_scan, 0, msgT))])

            f_stats1, f_vars1, f_inverse1 = layer_norm_stages(0, f_mm, st1, f_st1, var1, part1, f_part1, f_var1, sd1, f_sd1, r1, f_r1,
                                                              f_n1, lambda c: b_4[c.q4])
            f_stats2, f_vars2, f_inverse2 = layer_norm_stages(0, f_z, st2, f_st2, var2, part2, f_part2, f_var2, sd2, f_sd2, r2, f_r2,
                                                              f_o, lambda c: z4[c.q], mean2)

            def f_residual(c):
                wait(dve, f_n1T, c.n + 1)
                wait(dve, f_v, c.n - 1)
                v.scalar_tensor_tensor(out=u4[c.q], in0=b_t[:, :], scalar=col(GAM), in1=x1T[c.q4],
                                       op0=ALU.mult, op1=ALU.add).then_inc(f_u, 1)

            def f_sum(c):
                wait(dve, f_vT, c.n + 1)
                wait(dve, f_xload[c.q], 16 * (c.half + 1))
                wait(dve, f_o, c.n - 1)
                v.tensor_tensor(z4[c.q], b_3[:, :], x1_in[c.q], ALU.add).then_inc(f_z, 1)

            sweep(dve, CHUNKS, [(2, f_stats1), (2, f_vars1), (3, f_residual), (2, f_inverse1), (4, f_sum), (4, f_stats2),
                                (5, f_inverse2), (4, f_vars2), (5, shift_stage(mean2, r2, f_r2, f_shift))], unroll=4)

        @block.tensor
        def _(pe):
            t = nc.tensor

            def turn(target, source):
                for j in range(TILES):
                    last = t.transpose(tile(target, j), tile(source, j), ident[:, :])
                return last

            def linear(target, hT, m, weights, more=()):
                t.matmul(tiles(target[:, :]), pick[:, :], bias3[:, m, :].unsqueeze(1).to_broadcast([P, TILES, D]),
                         start=True, stop=False)
                pairs = [(hT, weights), *more]
                for j in range(TILES):
                    for k, (lhs, w) in enumerate(pairs):
                        last = t.matmul(tile(target, j), tile(lhs, j), w, start=False,
                                        stop=(j == TILES - 1 and k == len(pairs) - 1))
                return last

            pe.wait_ge(s_consts, 9)
            pe.wait_ge(s_params, 16 * N_PARAMS)
            for m in range(9):
                last = t.transpose(bank[m // 3][:, (m % 3) * P:(m % 3 + 1) * P], w_rows[:, m * D:(m + 1) * D],
                                   ident[:, :])
            last.then_inc(s_setup_pe, 1)
            pe.wait_ge(s_setup_dve, 3)
            for u in range(2):
                t.transpose(bank[3][:, u * P:(u + 1) * P], src_f[:, u, :], ident[:, :])
                t.transpose(bank[3][:, (2 + u) * P:(3 + u) * P], end_f[:, u, :], ident[:, :])
            t.transpose(bank[4][:, 0:P], v_rows, ident[:, :])
            for u in range(2):
                last = t.matmul(bank[5][0:1, 0:CHUNKS], ones[:, 0:1], reach[:, u * P:u * P + CHUNKS],
                                start=(u == 0), stop=(u == 1))
            last.then_inc(s_setup_pe, 1)
            pe.wait_ge(s_setup_dve, 5)

            for l in range(LAYERS):
                eb, base = ECHUNKS * l, CHUNKS * l

                def edge_turn(c):
                    wait(pe, s_gath[c.q], 64 * (EVEN[c.q] * l + c.half + 1))
                    wait(pe, e_gT, eb + c.n - 1)
                    turn(bank[c.q], gathered[c.q]).then_inc(e_gT_psum, 1)

                def edge_back(c):
                    wait(pe, e_scan, eb + c.n + 1)
                    wait(pe, e_y, eb + c.n - 1)
                    turn(bank[2 + c.q], yT[c.q]).then_inc(e_yT_psum, 1)

                stages = [(0, edge_turn), (1, edge_back)]
                if l == 0:
                    def count_turn(c):
                        wait(pe, s_count, c.n + 1)
                        for j in range(TILES):
                            last = t.matmul(bank[4][:, bass.ds(c.n * TILES + j, 1)], tile(count[c.q], j)[0:1, :],
                                            ones[0:1, 0:1], start=True, stop=True)
                        last.then_inc(s_count_pe, 1)
                    stages.append((1, count_turn))
                sweep(pe, ECHUNKS, stages)
                if l == 0:
                    pe.wait_ge(s_inv, 1)
                pe.wait_ge(e_y, eb + ECHUNKS)

                def rows_turn(c):
                    loads = 16 * (PAIRS * l + c.half + 1)
                    wait(pe, s_hload[c.q], loads)
                    wait(pe, d_xT, base + c.n)
                    turn(b_x, h_in[:, c.q, :])
                    wait(pe, s_aload[c.q], loads)
                    wait(pe, d_h0, base + c.n)
                    turn(b_a, a_in[:, c.q, :]).then_inc(d_turned, 1)

                def mm1(c):
                    wait(pe, d_h0, base + c.n + 1)
                    wait(pe, d_n1, base + c.n - 1)
                    linear(b_1[c.q], h0T[c.q], 3 * l, linT[:, 3 * l, :]).then_inc(d_mm1, 1)

                def turn1(c):
                    wait(pe, d_n1, base + c.n + 1)
                    wait(pe, d_h1, base + c.n)
                    wait(pe, d_h2, base + c.n - 3)
                    turn(b_t, n1[c.q]).then_inc(d_n1T, 1)

                def mm2(c):
                    wait(pe, d_h1, base + c.n + 1)
                    wait(pe, d_n2, base + c.n - 1)
                    linear(b_2[c.q], h1T[c.q], 3 * l + 1, linT[:, 3 * l + 1, :]).then_inc(d_mm2, 1)

                def turn2(c):
                    wait(pe, d_n2, base + c.n + 1)
                    ahead = min(c.n + 4, CHUNKS) if c.fixed else c.n + 4
                    wait(pe, d_h1, base + ahead)
                    if c.fixed:
                        wait(pe, d_h2, base + c.n)
                    turn(b_t, n2[c.q]).then_inc(d_n2T, 1)

                def mm3(c):
                    wait(pe, d_h2, base + c.n + 1)
                    wait(pe, d_o, base + c.n)
                    linear(b_3, h2T[c.q], 3 * l + 2, linT[:, 3 * l + 2, :]).then_inc(d_mm3, 1)

                sweep(pe, CHUNKS, [(0, rows_turn), (1, mm1), (2, turn1), (3, mm2), (5, turn2), (6, mm3)])

                for k in range(2):
                    pe.wait_ge(s_total_act, 3 * l + 1 + k)
                    t.matmul(bank[0][:, k:k + 1], ones[:, :], tot[:, 3 * k:3 * k + 1], start=True, stop=True
                             ).then_inc(s_total_pe, 1)
            pe.wait_ge(s_gn, LAYERS)

            def y_turn(c):
                wait(pe, y_hload[c.q], 16 * (c.half + 1))
                wait(pe, y_xT, c.n)
                turn(b_x, h_in[:, c.q, :]).then_inc(y_turned, 1)

            def y_turn_back(c):
                wait(pe, y_xT, c.n + 1)
                wait(pe, y_z, c.n - 1)
                turn(b_1[c.q], xT[c.q]).then_inc(y_back, 1)

            sweep(pe, CHUNKS, [(0, y_turn), (1, y_turn_back)])

            def m_turn(c):
                wait(pe, m_attr[c.q], 16 * (c.half + 1))
                wait(pe, m_aT, c.n - 1)
                turn(bank[2 + c.q], attr_in[c.q]).then_inc(m_aT_psum, 1)
                wait(pe, s_gath[c.q], 64 * (EVEN[c.q] * LAYERS + c.half + 1))
                wait(pe, m_gT, c.n - 1)
                turn(bank[c.q], gathered[c.q]).then_inc(m_gT_psum, 1)

            def m_matmul(c):
                wait(pe, m_gT, c.n + 1)
                wait(pe, m_aT, c.n + 1)
                wait(pe, m_msg, c.n - 1)
                t.matmul(bank[4 + c.q][:, :], w_msg[:, 0, :], gT[c.q], start=True, stop=False)
                t.matmul(bank[4 + c.q][:, :], w_msg[:, 1, :], attrT[c.q], start=False, stop=True).then_inc(m_mm, 1)

            def m_back(c):
                wait(pe, m_scan, c.n + 1)
                wait(pe, m_y, c.n - 1)
                turn(bank[6 + c.q], yT[c.q]).then_inc(m_yT_psum, 1)

            pe.wait_ge(y_z, CHUNKS)
            sweep(pe, ECHUNKS, [(0, m_turn), (1, m_matmul), (2, m_back)])
            pe.wait_ge(m_y, ECHUNKS)

            def f_turn(c):
                wait(pe, f_hload[c.q], 16 * (c.half + 1))
                wait(pe, f_xT, c.n)
                turn(b_x, h_in[:, c.q, :])
                wait(pe, f_aload[c.q], 16 * (c.half + 1))
                wait(pe, f_aT, c.n)
                turn(b_a, a_in[:, c.q, :]).then_inc(f_turned, 1)

            def f_matmul(c):
                wait(pe, f_aT, c.n + 1)
                wait(pe, f_n1, c.n - 3)
                linear(b_4[c.q4], x1T[c.q4], 9, w_upd[:, 0, :], [(meanT4[c.q], w_upd[:, 1, :])]).then_inc(f_mm, 1)

            def f_turn1(c):
                wait(pe, f_n1, c.n + 1)
                wait(pe, f_u, c.n)
                turn(b_t, n4[c.q]).then_inc(f_n1T, 1)

            def f_turn2(c):
                wait(pe, f_v, c.n + 1)
                wait(pe, f_z, c.n)
                turn(b_3, v4[c.q]).then_inc(f_vT, 1)

            sweep(pe, CHUNKS, [(0, f_turn), (4, f_turn2), (1, f_matmul), (2, f_turn1)], unroll=4)


_INS = ["x", "src", "dst", "edge_attr_128", "L0_gnn_W", "L0_gnn_b", "L0_gnn_mlp_ln_w", "L0_gnn_mlp_ln_b",
        "L0_gnn_eps", "L0_gnn_out_ln_w", "L0_gnn_out_ln_b", "L1_gnn_W_msg", "L1_gnn_b_msg", "L1_gnn_W_upd",
        "L1_gnn_b_upd", "L1_gnn_gamma", "L1_gnn_beta"]


def kernel(**inputs):
    import numpy as _np
    import concourse.bacc as _bacc
    from concourse import mybir as _mybir
    from concourse.bass_utils import run_bass_kernel_spmd as _run

    nc = _bacc.Bacc("TRN2", target_bir_lowering=False, num_devices=1)
    arrays, args = {}, []
    for name in _INS:
        a = _np.ascontiguousarray(inputs[name])
        arrays[f"in_{name}"] = a
        args.append(nc.dram_tensor(f"in_{name}", a.shape, _mybir.dt.from_np(a.dtype), kind="ExternalInput").ap())
    args.append(nc.dram_tensor("out_rows_dram", (N, D), F32, kind="ExternalOutput").ap())
    build(nc, *args)
    r = _run(nc, [arrays], core_ids=[0])
    return r.results[0]["out_rows_dram"]
```

```python
from contextlib import ExitStack

import concourse.bass as bass
from concourse import mybir

F32 = mybir.dt.float32
BF16 = mybir.dt.bfloat16
I32 = mybir.dt.int32
U8 = mybir.dt.uint8
ALU = mybir.AluOpType
ACT = mybir.ActivationFunctionType
AXX = mybir.AxisListType.X

N, E, D, LAYERS = 50000, 25000, 128, 3
P = 128
TILES = 4
ROWS = P * TILES
CHUNKS = -(-N // ROWS)
NPAD = CHUNKS * ROWS
TAIL = (N - (CHUNKS - 1) * ROWS) // TILES
ECHUNKS = -(-E // ROWS)
EPAD = ECHUNKS * ROWS
ETILES = EPAD // P
HALF = ETILES // 2
FULLROWS = E // P - HALF
REST = E % P
NOWHERE = 1 << 20
SPARE = NPAD
SPARES = 4 * ROWS
NODES = CHUNKS // ECHUNKS
EPS = 1e-5
STATGROUP = ROWS // 2
PIECES = 7
PIECE = EPAD // PIECES
RANK_STEPS = 2 * PIECES + 4
EVEN = [(ECHUNKS + 1) // 2, ECHUNKS // 2]
EQUADS = [(ECHUNKS + 3 - q) // 4 for q in range(4)]
PAIRS = CHUNKS // 2
QUADS = [(CHUNKS + 3 - q) // 4 for q in range(4)]


class Chunk:

    def __init__(self, n, half, fourth, const, fixed):
        self.n, self.half, self.fixed = n, half, fixed
        self.q, self.q4, self.q8 = const % 2, const % 4, const % 8
        self.pair = self.q4 // 2
        self.closes = self.q == 1
        self.fourth = fourth

    def of_pair(self, values):
        return values[:, self.pair, self.q * TILES:(self.q + 1) * TILES]

    def is_(self, value):
        return self.fixed and self.n == value


def sweep(eng, count, stages, unroll=2):
    deepest = max(lag for lag, _ in stages)
    lead = -(-(deepest + unroll) // unroll) * unroll
    blocks = (count - 1) // unroll

    def peeled(t):
        for lag, stage in stages:
            c = t - lag
            if 0 <= c < count:
                stage(Chunk(c, c // 2, c // 4, c, True))

    for t in range(lead):
        peeled(t)
    with eng.Fori(lead // unroll, blocks) as k:
        for r in range(unroll):
            for lag, stage in stages:
                const = r - lag
                fourth = k * (unroll // 4) + const // 4 if unroll % 4 == 0 else None
                stage(Chunk(k * unroll + const, k * (unroll // 2) + const // 2, fourth, const, False))
    for t in range(blocks * unroll, count + deepest):
        peeled(t)


def wait(eng, sem, value):
    if isinstance(value, int) and value <= 0:
        return
    eng.wait_ge(sem, value)


def quarter(c):
    return 16 * c.fourth


def build(nc, x, src, dst, edge_attr_128, L0_gnn_W, L0_gnn_b, L0_gnn_mlp_ln_w, L0_gnn_mlp_ln_b,
          L0_gnn_eps, L0_gnn_out_ln_w, L0_gnn_out_ln_b, L1_gnn_W_msg, L1_gnn_b_msg, L1_gnn_W_upd,
          L1_gnn_b_upd, L1_gnn_gamma, L1_gnn_beta, out):
    ctx = ExitStack()
    with ctx:
        def sb(name, shape, dt=F32):
            return ctx.enter_context(nc.sbuf_tensor(name, shape, dt))

        def sem(name):
            return ctx.enter_context(nc.semaphore(name))

        def sems(name, n=2):
            return [sem(f"{name}{i}") for i in range(n)]

        act_rows = nc.dram_tensor("act_rows", [NPAD, D], F32).ap()
        x1_rows = nc.dram_tensor("x1_rows", [NPAD, D], F32).ap()
        pre = nc.dram_tensor("pre", [SPARE + SPARES, D], F32).ap()
        attr_rows = nc.dram_tensor("attr_rows", [EPAD, D], F32).ap()
        same_row = nc.dram_tensor("same_row", [1, EPAD + 1], U8).ap()

        def chunks_of(t):
            return t.rearrange("(c p j) f -> c p (j f)", p=P, j=TILES)

        act_c, x1_c, pre_c = chunks_of(act_rows), chunks_of(x1_rows), chunks_of(pre[0:NPAD, :])
        WHOLE = (CHUNKS - 1) * ROWS
        x_c = chunks_of(x[0:WHOLE, :])
        x_tail = x[WHOLE:N, :].rearrange("(p j) f -> p (j f)", j=TILES)
        out_c = chunks_of(out[0:WHOLE, :])
        out_tail = out[WHOLE:N, :].rearrange("(p j) f -> p (j f)", j=TILES)
        src_padded = nc.dram_tensor("src_padded", [EPAD, 1], I32).ap()
        dst_padded = nc.dram_tensor("dst_padded", [EPAD, 1], I32).ap()
        src_sorted = nc.dram_tensor("src_sorted", [EPAD, 1], I32).ap()
        dst_sorted = nc.dram_tensor("dst_sorted", [EPAD, 1], I32).ap()

        ident = sb("ident", [P, P])
        ones = sb("ones", [P, P])
        pick = sb("pick", [P, P], BF16)
        zeros = sb("zeros", [P, D])
        FILL = NPAD * D // P // ECHUNKS
        fill = sb("fill", [P, FILL])
        b_pre = sb("b_pre", [P, LAYERS + 1, D])
        lin1x = sb("lin1x", [P, LAYERS, D])
        onerow = sb("onerow", [P, ROWS], BF16)
        linT = sb("linT", [P, 9, D])
        w_msg = sb("w_msg", [P, 2, D])
        w_upd = sb("w_upd", [P, 2, D])
        bias3 = sb("bias3", [P, 2 * LAYERS, D], BF16)
        cols = sb("cols", [P, P])
        eps1 = sb("eps1", [P, LAYERS])
        epsc = sb("epsc", [P, 1])
        src_tab = sb("src_tab", [P, ETILES], I32)
        end_tab = sb("end_tab", [P, ETILES], I32)
        inv_tab = sb("inv_tab", [P, ETILES])
        same = sb("same", [P, EPAD], U8)
        need_row = sb("need_row", [1, CHUNKS], I32)
        descents = sb("descents", [P, 1])
        unsorted = sb("unsorted", [1, 1], I32)
        col_in = sb("col_in", [P, 2, 2], I32)
        dst_f32 = sb("dst_f32", [P, 2])
        rank_part = sb("rank_part", [P, 2, 8])
        rank = sb("rank", [P, 2], I32)
        sums = sb("sums", [P, ECHUNKS, ROWS])
        h_in = sb("h_in", [P, 2, ROWS])
        a_in = sb("a_in", [P, 2, ROWS])
        work = sb("work", [P, 22, ROWS])
        sum_out = sb("sum_out", [P, 2, ROWS])
        src_now = sb("src_now", [P, 4, TILES], I32)
        end_now = sb("end_now", [P, 2, TILES], I32)
        st1 = sb("st1", [P, 4, TILES, 6])
        st2 = sb("st2", [P, 4, TILES, 6])
        var1 = sb("var1", [P, 2, 2 * TILES])
        var2 = sb("var2", [P, 2, 2 * TILES])
        part1 = sb("part1", [P, 2, 4, 2 * TILES])
        part2 = sb("part2", [P, 2, 4, 2 * TILES])
        mean1 = sb("mean1", [P, 2, 2 * TILES])
        mean2 = sb("mean2", [P, 2, 2 * TILES])
        shift = sb("shift", [P, 2, 2 * TILES])
        sd1 = sb("sd1", [P, 2, 2 * TILES])
        sd2 = sb("sd2", [P, 2, 2 * TILES])
        r1 = sb("r1", [P, 2, 2 * TILES])
        r2 = sb("r2", [P, 2, 2 * TILES])
        st3 = sb("st3", [P, CHUNKS, 6])
        dev = sb("dev", [P, CHUNKS, 2])
        valid = sb("valid", [P, 1])
        tot = sb("tot", [P, 8])
        gn_scale = sb("gn_scale", [P, LAYERS])
        gn_bias = sb("gn_bias", [P, LAYERS])

        def ring(first, n=2):
            return [work[:, first + i, :] for i in range(n)]

        n1, h1T, n2, h2T, o_rows = (ring(4 * i, 4) for i in range(5))
        node_in = [a_in[:, 0, :], a_in[:, 1, :], h_in[:, 0, :], h_in[:, 1, :]]
        xT, pre_rows = ring(0), ring(18, 4)
        gathered, gT, yT = ring(2, 4), ring(6), ring(8)
        attr_in, attrT, msgT, count = (ring(2 * i) for i in (5, 6, 7, 8))
        y_in, x_in, z1, y_rows = ring(2, 4), ring(6, 4), ring(10, 4), ring(14, 4)
        x1T, s4, n4, u4, v4, out_rows = ring(0, 8), ring(8, 4), ring(12), ring(14), ring(16), ring(18, 4)

        idx_rows = work[:, 0:2, :].rearrange("p a b -> p (a b)").bitcast(I32)
        idx_f = work[:, 2:4, :].rearrange("p a b -> p (a b)")
        w_rows = work[:, 4:7, :].rearrange("p a b -> p (a b)")[:, 0:9 * D]
        b_rows = work[:, 10:13, :].rearrange("p a b -> p (a b)")[:, 0:10 * D]
        b_part = work[:, 13:15, :].rearrange("p a b -> p (a b)")[:, 0:6 * D].rearrange("p (l f) -> p l f", l=LAYERS)
        v_rows = work[:, 13, 0:P]
        thr_i = work[:, 14, 0:CHUNKS].bitcast(I32)
        thr = work[:, 14, P:P + CHUNKS]
        reach = work[:, 15, 0:2 * P]
        b_bf = work[:, 15, :].bitcast(BF16)[:, 0:6 * D].rearrange(
            "p (l f) -> p l f", l=LAYERS)
        means9 = work[:, 18, 0:32]
        same_rows = work[:, 19, 0:64].bitcast(U8)
        spare_i = work[:, 20, 0:2 * P].bitcast(I32).rearrange("p (u e) -> p u e", u=2)
        spare = work[:, 21, 0:2 * P].rearrange("p (u e) -> p u e", u=2)
        row_kept = work[:, 21, 2 * P:4 * P].rearrange("p (u e) -> p u e", u=2)

        def idx_block(t, k):
            return t[:, k * 2 * P:(k + 1) * 2 * P].rearrange("p (u e) -> p u e", u=2)

        src_i, dst_i, nxt_i = (idx_block(idx_rows, k) for k in range(3))
        src_f, dst_f, nxt_f, end_f = (idx_block(idx_f, k) for k in range(4))

        all_dst = sums[:, :, :].rearrange("p c e -> p (c e)")
        goes_before = [t[:, :, :].rearrange("p a b -> p (a b)").bitcast(U8)[:, 0:PIECE] for t in (h_in, a_in)]
        triangle = fill[:, 0:P]
        attr_tile = [sum_out[:, q, 0:D] for q in range(2)]

        bank = [ctx.enter_context(nc.psum_tensor(f"bank{i}", [P, ROWS], F32)) for i in range(8)]
        b_gT, b_back, b_xT, b_pre_rows = bank[0:2], bank[2], [bank[3], bank[5]], bank[6:8]
        b_count = bank[4]
        b_t1, b_t2, b_3, b_2 = bank[0], bank[1], bank[2:4], bank[4:8]
        b_x, b_1 = bank[0:2], bank[4:8]
        b_n, b_p, b_z = bank[2], bank[3], bank[4:8]

        LNW, LNB, OW, OB, GAM, BET, BMSG = 0, 6, 12, 15, 18, 19, 20

        def col(i):
            return cols[:, i:i + 1]

        def tiles(ap):
            return ap.rearrange("p (j f) -> p j f", j=TILES)

        def tile(ap, j):
            return ap[:, j * P:(j + 1) * P]

        s_consts, s_prefilled, s_idx, s_params, s_same_out, s_same_in = (
            sem(n) for n in ("consts", "index_rows_prefilled", "idx_loaded", "params_loaded", "same_stored",
                             "same_loaded"))
        s_setup_dve, s_setup_pe, s_setup_act = sem("setup_dve"), sem("setup_pe"), sem("setup_act")
        s_filled, s_fill_row = sem("pre_filled"), sem("fill_row_set")
        s_descents, s_descents_pe, s_unsorted = sem("descents"), sem("descents_summed"), sem("unsorted_known")
        o_padded, o_all_dst, o_triangle, o_step, o_ranked = (
            sem(n) for n in ("edges_padded", "all_dst_loaded", "triangle_set", "rank_step", "tile_ranked"))
        o_tile, o_placed = sems("tile_loaded"), sems("tile_placed")
        s_src_now, s_end_now, s_tick = sem("src_now_set"), sem("end_now_set"), sem("pool_tick")
        s_gath = sems("rows_gathered", 4)
        s_scat = sems("rows_scattered")
        s_scattered = sem("tiles_scattered")
        e_gT_psum, e_gT, e_scan, e_yT_psum, e_y = (
            sem(n) for n in ("edge_rows_turned", "edge_gT", "edge_scanned", "edge_sums_turned", "edge_sums_kept"))
        s_hload, s_aload, s_store = sems("h_loaded", 4), sems("pre_loaded", 4), sems("rows_stored", 4)
        s_pre_store = sems("pre_stored", 4)
        e_turned, e_xT, e_pre, e_mm1, d_st1, d_var1, d_sd1, d_r1, d_n1, d_n1T, d_h1 = (
            sem(n) for n in ("e_turned", "e_xT", "e_pre", "e_mm1", "d_st1", "d_var1", "d_sd1", "d_r1", "d_n1",
                             "d_n1T", "d_h1"))
        d_mm2, d_st2, d_var2, d_sd2, d_r2, d_n2, d_n2T, d_h2, d_mm3, d_o, d_ost = (
            sem(n) for n in ("d_mm2", "d_st2", "d_var2", "d_sd2", "d_r2", "d_n2", "d_n2T", "d_h2", "d_mm3", "d_o",
                             "d_ost"))
        d_part1, d_part2, y_part, f_part1, f_part2 = (
            sem(n) for n in ("d_part1", "d_part2", "y_part", "f_part1", "f_part2"))
        y_shift, f_shift = sem("y_shift"), sem("f_shift")
        s_chain, s_total_pe, s_total_act, s_gn = (
            sem(n) for n in ("dve_chain", "total_pe", "total_act", "graph_norm_ready"))
        y_hload, y_xload, y_store = sems("y_h_loaded", 4), sems("y_x_loaded", 4), sems("x1_stored", 4)
        y_turned, y_xT, y_back, y_z, y_st, y_var, y_sd, y_r, y_o = (
            sem(n) for n in ("y_turned", "y_xT", "y_back", "y_z", "y_st", "y_var", "y_sd", "y_r", "y_o"))
        m_attr = sems("attr_loaded")
        m_gT_psum, m_aT_psum, m_gT, m_aT, m_mm, m_msg, m_scan, m_yT_psum, m_y = (
            sem(n) for n in ("m_gT_psum", "m_aT_psum", "m_gT", "m_aT", "m_mm", "m_msg", "m_scan", "m_yT_psum", "m_y"))
        s_count, s_count_pe, s_inv = sem("counted"), sem("counts_turned"), sem("inv_ready")
        f_hload, f_aload, f_store = sems("f_h_loaded"), sems("f_a_loaded"), sems("out_stored", 4)
        (f_turned, f_xT, f_sum, f_mm, f_st1, f_var1, f_sd1, f_r1, f_n1, f_n1T, f_u, f_v, f_z, f_st2, f_var2,
         f_sd2, f_r2, f_o) = (
            sem("f_" + n) for n in ("turned", "xT", "sum", "mm", "st1", "var1", "sd1", "r1", "n1", "n1T", "u", "v",
                                    "z", "st2", "var2", "sd2", "r2", "o"))
        N_PARAMS = 13

        block = ctx.enter_context(nc.Block())

        @block.sync
        def _(sp):
            def load_indices(src, dst):
                for table, rows, shift in ((src, src_i, 0), (dst, dst_i, 0), (dst, nxt_i, 1)):
                    first = HALF * P
                    second = FULLROWS * P
                    sp.dma_start(rows[0:HALF, 0, :],
                                 table[shift:shift + first].rearrange("(t e) -> t e", e=P)).then_inc(s_idx, 16)
                    sp.dma_start(rows[0:FULLROWS, 1, :],
                                 table[shift + first:shift + first + second].rearrange("(t e) -> t e", e=P)
                                 ).then_inc(s_idx, 16)
                    sp.dma_start(rows[FULLROWS:FULLROWS + 1, 1, 0:REST - shift],
                                 table[shift + first + second:E].unsqueeze(0)).then_inc(s_idx, 16)

            sp.wait_ge(s_prefilled, 1)
            load_indices(src, dst)
            sp.wait_ge(s_consts, 6)
            sp.dma_start(w_rows.rearrange("p (m k) -> p m k", k=D),
                         L0_gnn_W.rearrange("l i o k -> o (l i) k")).then_inc(s_params, 16)
            sp.dma_start(b_rows[:, 0:9 * D],
                         L0_gnn_b.rearrange("l i o -> (l i o)").partition_broadcast(P)).then_inc(s_params, 16)
            sp.dma_start(b_rows[:, 9 * D:10 * D], L1_gnn_b_upd.partition_broadcast(P)).then_inc(s_params, 16)
            sp.dma_start(w_msg[:, :, :], L1_gnn_W_msg.rearrange("(h k) f -> k h f", k=P)).then_inc(s_params, 16)
            sp.dma_start(w_upd[:, :, :], L1_gnn_W_upd.rearrange("(h k) f -> k h f", k=P)).then_inc(s_params, 16)
            for at, rows in ((LNW, L0_gnn_mlp_ln_w.rearrange("l i f -> (l i) f")),
                             (LNB, L0_gnn_mlp_ln_b.rearrange("l i f -> (l i) f")),
                             (OW, L0_gnn_out_ln_w), (OB, L0_gnn_out_ln_b), (GAM, L1_gnn_gamma.unsqueeze(0)),
                             (BET, L1_gnn_beta.unsqueeze(0)), (BMSG, L1_gnn_b_msg.unsqueeze(0))):
                if at == OW:
                    sp.dma_start(eps1[:, :], L0_gnn_eps.partition_broadcast(P)).then_inc(s_params, 16)
                sp.dma_start(v_rows[at:at + rows.shape[0], :], rows).then_inc(s_params, 16)

            def load_tile(c):
                wait(sp, o_placed[c.q], 48 * c.half)
                for i, rows in enumerate((src_padded, dst_padded)):
                    sp.dma_start(col_in[:, c.q, i:i + 1], rows[bass.ds(c.n * P, P), :]).then_inc(o_tile[c.q], 16)
                if c.is_(ETILES - 1):
                    sp.dma_start(attr_tile[c.q][0:REST, :], edge_attr_128[E - REST:E, :]).then_inc(o_tile[c.q], 16)
                else:
                    sp.dma_start(attr_tile[c.q], edge_attr_128[bass.ds(c.n * P, P), :]).then_inc(o_tile[c.q], 16)

            sp.wait_ge(s_unsorted, 1)
            out_of_order = sp.value_load(unsorted[0:1, 0:1], min_val=0, max_val=E)
            with sp.If(out_of_order > 0):
                for rows, padded in ((src_i, src_padded), (dst_i, dst_padded)):
                    for u in range(2):
                        sp.dma_start(padded[u * HALF * P:(u + 1) * HALF * P, :].rearrange("(t e) o -> t (e o)", e=P),
                                     rows[0:HALF, u, :]).then_inc(o_padded, 16)
                sp.wait_ge(o_padded, 64)
                sp.dma_start(all_dst.bitcast(I32), dst_padded[:, 0].partition_broadcast(P)).then_inc(o_all_dst, 16)
                sweep(sp, ETILES, [(0, load_tile)])
                for q in range(2):
                    sp.wait_ge(o_placed[q], 48 * ETILES // 2)
                load_indices(src_sorted[:, 0], dst_sorted[:, 0])
            with sp.Else():
                sp.wait_ge(s_unsorted, 1)
            sp.wait_ge(s_setup_dve, 3)
            sp.dma_start(same_row[0:1, 0:1], zeros[0:1, 0:1].bitcast(U8)[:, 0:1]).then_inc(s_same_out, 16)
            for u in range(2):
                sp.dma_start(same_row[0, 1 + u * HALF * P:1 + (u + 1) * HALF * P].rearrange("(t e) -> t e", e=P),
                             same_rows.rearrange("p (u e) -> p u e", u=2)[0:HALF, u, :]).then_inc(s_same_out, 16)
            sp.wait_ge(s_same_out, 48)
            sp.dma_start(same[:, :], same_row[0, 0:EPAD].partition_broadcast(P)).then_inc(s_same_in, 16)
            every_row = pre[0:NPAD, :].rearrange("(p k r) f -> k p (r f)", p=P, k=ECHUNKS)
            def refill(c):
                wait(sp, m_gT_psum, c.n)
                sp.dma_start(every_row[bass.ds(c.n, 1), :, :].squeeze(0), fill[:, :]).then_inc(s_filled, 16)

            for l in range(LAYERS):
                base = CHUNKS * l
                for q in range(4):
                    wait(sp, s_store[q], 16 * QUADS[q] * l)
                wait(sp, s_gn, l)

                def load_nodes(c):
                    for h in range(NODES):
                        n = c.n * NODES + h
                        r = c.q * NODES + h
                        wait(sp, e_turned, base + n - 3)
                        if l == 0 and c.is_(ECHUNKS - 1) and h == NODES - 1:
                            sp.dma_start(node_in[r][0:TAIL, :], x_tail).then_inc(s_hload[r], 16)
                        else:
                            rows = x_c if l == 0 else act_c
                            sp.dma_start(node_in[r], rows[bass.ds(n, 1), :, :].squeeze(0)).then_inc(s_hload[r], 16)

                def store_pre(c):
                    for h in range(NODES):
                        n = c.n * NODES + h
                        wait(sp, e_pre, base + n + 1)
                        sp.dma_start(pre_c[bass.ds(n, 1), :, :].squeeze(0), pre_rows[c.q * NODES + h]
                                     ).then_inc(s_pre_store[c.q * NODES + h], 16)

                if l == 0:
                    sp.wait_ge(s_fill_row, 1)
                    for i in range(2):
                        rows = pre[SPARE + i * SPARES // 2:SPARE + (i + 1) * SPARES // 2, :]
                        sp.dma_start(rows.rearrange("(p r) f -> p (r f)", p=P), fill[:, 0:SPARES * D // (2 * P)]
                                     ).then_inc(s_filled, 16)
                sweep(sp, ECHUNKS, [(0, load_nodes), (3, store_pre)])

                def load_pre(c):
                    wait(sp, d_n1, base + c.n - 3)
                    need = sp.value_load(need_row[0:1, bass.ds(c.n, 1)], min_val=0, max_val=ETILES)
                    sp.wait_ge(s_scattered, need + (ETILES * l + 1))
                    sp.dma_start(node_in[c.q4], pre_c[bass.ds(c.n, 1), :, :].squeeze(0)).then_inc(s_aload[c.q4], 16)

                def store_act(c):
                    wait(sp, d_o, base + c.n + 1)
                    sp.dma_start(act_c[bass.ds(c.n, 1), :, :].squeeze(0), o_rows[c.q4]).then_inc(s_store[c.q4], 16)

                if l == 0:
                    sp.wait_ge(s_setup_dve, 4)
                for q in range(2):
                    for h in range(NODES):
                        sp.wait_ge(s_pre_store[q * NODES + h], 16 * EVEN[q] * (l + 1))
                sweep(sp, CHUNKS, [(0, load_pre), (12, store_act)], unroll=4)

            for q in range(4):
                sp.wait_ge(s_store[q], 16 * QUADS[q] * LAYERS)
            sp.wait_ge(s_gn, LAYERS)

            def load_y(c):
                wait(sp, y_turned, c.n - 3)
                sp.dma_start(y_in[c.q4], act_c[bass.ds(c.n, 1), :, :].squeeze(0)).then_inc(y_hload[c.q4], 16)

            def load_x(c):
                wait(sp, y_z, c.n - 3)
                if c.is_(CHUNKS - 1):
                    sp.dma_start(x_in[c.q4][0:TAIL, :], x_tail).then_inc(y_xload[c.q4], 16)
                else:
                    sp.dma_start(x_in[c.q4], x_c[bass.ds(c.n, 1), :, :].squeeze(0)).then_inc(y_xload[c.q4], 16)

            def store_y(c):
                wait(sp, y_o, c.n + 1)
                sp.dma_start(x1_c[bass.ds(c.n, 1), :, :].squeeze(0), y_rows[c.q4]).then_inc(y_store[c.q4], 16)

            sweep(sp, CHUNKS, [(0, load_y), (1, load_x), (7, store_y)], unroll=4)

            for q in range(4):
                sp.wait_ge(y_store[q], 16 * QUADS[q])

            def load_attr(source):
                whole = source[0:(ECHUNKS - 1) * ROWS, :].rearrange("(c j p) f -> c p j f", j=TILES, p=P)
                rest = source[(ECHUNKS - 1) * ROWS:E - REST, :].rearrange("(j p) f -> p j f", p=P)

                def stage(c):
                    wait(sp, m_aT_psum, c.n - 1)
                    if c.is_(ECHUNKS - 1):
                        sp.dma_start(tiles(attr_in[c.q])[:, 0:TILES - 1, :], rest).then_inc(m_attr[c.q], 16)
                        sp.dma_start(tile(attr_in[c.q], TILES - 1)[0:REST, :], source[E - REST:E, :]
                                     ).then_inc(m_attr[c.q], 16)
                    else:
                        sp.dma_start(tiles(attr_in[c.q]), whole[bass.ds(c.n, 1), :, :, :].squeeze(0)
                                     ).then_inc(m_attr[c.q], 16)
                return stage

            sp.wait_ge(s_fill_row, 2)
            with sp.If(out_of_order > 0):
                sweep(sp, ECHUNKS, [(0, load_attr(attr_rows)), (0, refill)])
            with sp.Else():
                sweep(sp, ECHUNKS, [(0, load_attr(edge_attr_128)), (0, refill)])
            sp.wait_ge(m_y, ECHUNKS)

            def load_f(c):
                wait(sp, f_turned, c.n - 1)
                sp.dma_start(h_in[:, c.q, :], x1_c[bass.ds(c.n, 1), :, :].squeeze(0)).then_inc(f_hload[c.q], 16)

            def load_means(c):
                wait(sp, f_sum, c.n - 1)
                need = sp.value_load(need_row[0:1, bass.ds(c.n, 1)], min_val=0, max_val=ETILES)
                sp.wait_ge(s_scattered, need + (ETILES * LAYERS + 1))
                sp.dma_start(a_in[:, c.q, :], pre_c[bass.ds(c.n, 1), :, :].squeeze(0)).then_inc(f_aload[c.q], 16)

            def store_out(c):
                wait(sp, f_o, c.n + 1)
                if c.is_(CHUNKS - 1):
                    sp.dma_start(out_tail, out_rows[c.q4][0:TAIL, :]).then_inc(f_store[c.q4], 16)
                else:
                    sp.dma_start(out_c[bass.ds(c.n, 1), :, :].squeeze(0), out_rows[c.q4]).then_inc(f_store[c.q4], 16)

            sweep(sp, CHUNKS, [(0, load_f), (1, load_means), (10, store_out)], unroll=8)
            for q in range(4):
                sp.wait_ge(f_store[q], 16 * QUADS[q])

        @block.gpsimd
        def _(pool):
            g = nc.gpsimd
            last_row = g.to_reg(N - 1)
            last_spare = g.to_reg(SPARE + SPARES - 1)
            g.sem_inc(s_scattered, 1)
            g.memset(idx_rows[:, 0:3 * 2 * P], NOWHERE).then_inc(s_prefilled, 1)
            g.memset(zeros[:, :], 0.0).then_inc(s_consts, 1)
            g.memset(v_rows, 0.0).then_inc(s_consts, 1)
            g.memset(ones[:, :], 1.0).then_inc(s_consts, 1)
            g.memset(onerow[:, :], 1.0).then_inc(s_consts, 1)
            g.memset(epsc[:, :], EPS).then_inc(s_consts, 1)
            g.memset(ident[:, :], 0.0).then_inc(s_consts, 1)
            pool.wait_ge(s_consts, 6)
            g.affine_select(out=ident[:, :], in_=ident[:, :], compare_op=ALU.not_equal, fill=1.0, base=0,
                            pattern=[[-1, P]], channel_multiplier=1).then_inc(s_consts, 1)
            g.affine_select(out=valid[:, :], in_=ones[:, 0:1], compare_op=ALU.is_gt, fill=0.0, base=TAIL,
                            pattern=[[0, 1]], channel_multiplier=-1).then_inc(s_consts, 1)
            g.iota(thr_i, pattern=[[ROWS, CHUNKS]], base=ROWS, channel_multiplier=0).then_inc(s_consts, 1)
            g.iota(spare_i, pattern=[[HALF * P, 2], [1, P]], base=0, channel_multiplier=P).then_inc(s_consts, 1)

            def run_gathers(rows, phase):
                def stage(c):
                    wait(pool, s_src_now, ECHUNKS * phase + c.n + 1)
                    g.sem_inc(s_tick, 1)
                    for j in range(TILES):
                        g.indirect_dma_start(tile(gathered[c.q4], j), None, rows,
                                             bass.IndirectOffsetOnAxis(src_now[:, c.q4, j:j + 1], 0),
                                             bounds_check=last_row, oob_is_err=False).then_inc(s_gath[c.q4], 16)
                sweep(pool, ECHUNKS, [(0, stage)], unroll=4)

            def run_scatters(phase, kept, kept_base, ready):
                def stage(c):
                    wait(pool, kept, kept_base + c.n + 1)
                    g.sem_inc(s_tick, 1)
                    g.tensor_copy(end_now[:, c.q, :], end_tab[:, bass.ds(c.n * TILES, TILES)]).then_inc(s_end_now, 1)
                    g.tensor_copy(sum_out[:, c.q, :], sums[:, bass.ds(c.n, 1), :].squeeze(1)).then_inc(s_end_now, 1)
                    if c.is_(0):
                        ready()
                    else:
                        pool.wait_ge(s_scat[1 - c.q], 64 * (EVEN[1 - c.q] * phase + c.half + c.q))
                        g.sem_inc(s_scattered, TILES)
                    wait(pool, s_end_now, 2 * (ECHUNKS * phase + c.n + 1))
                    g.sem_inc(s_tick, 1)
                    for j in range(TILES):
                        how = (dict(bounds_check=last_spare, oob_is_err=True, compute_op=ALU.add) if phase < LAYERS
                               else dict(bounds_check=last_row, oob_is_err=False))
                        g.indirect_dma_start(pre, bass.IndirectOffsetOnAxis(end_now[:, c.q, j:j + 1], 0),
                                             tile(sum_out[:, c.q, :], j), None, **how).then_inc(s_scat[c.q], 16)
                sweep(pool, ECHUNKS, [(0, stage)])
                pool.wait_ge(s_scat[(ECHUNKS - 1) % 2], 64 * EVEN[(ECHUNKS - 1) % 2] * (phase + 1))
                g.sem_inc(s_scattered, TILES)

            last_edge = g.to_reg(EPAD - 1)

            def place_tile(c):
                wait(pool, o_ranked, c.n + 1)
                g.sem_inc(s_tick, 1)
                for rows, target in ((col_in[:, c.q, 0:1], src_sorted), (col_in[:, c.q, 1:2], dst_sorted),
                                     (attr_tile[c.q], attr_rows)):
                    g.indirect_dma_start(target, bass.IndirectOffsetOnAxis(rank[:, c.q:c.q + 1], 0), rows, None,
                                         bounds_check=last_edge, oob_is_err=False).then_inc(o_placed[c.q], 16)

            pool.wait_ge(s_unsorted, 1)
            out_of_order = pool.value_load(unsorted[0:1, 0:1], min_val=0, max_val=E)
            with pool.If(out_of_order > 0):
                g.affine_select(out=triangle, in_=ones[:, :], compare_op=ALU.is_gt, fill=0.0, base=0,
                                pattern=[[-1, P]], channel_multiplier=1).then_inc(o_triangle, 1)
                sweep(pool, ETILES, [(0, place_tile)])
            with pool.Else():
                g.sem_inc(s_tick, 1)
            pool.wait_ge(s_setup_dve, 4)
            for l in range(LAYERS):
                for q in range(4):
                    wait(pool, s_store[q], 16 * QUADS[q] * l)
                run_gathers(x if l == 0 else act_rows, l)

                def pre_is_stored():
                    pool.wait_ge(s_filled, 16 * 2)
                    for q in range(2):
                        for h in range(NODES):
                            pool.wait_ge(s_pre_store[q * NODES + h], 16 * EVEN[q] * (l + 1))

                run_scatters(l, e_y, ECHUNKS * l, pre_is_stored)
            for q in range(4):
                pool.wait_ge(y_store[q], 16 * QUADS[q])
            run_gathers(x1_rows, LAYERS)
            run_scatters(LAYERS, m_y, 0, lambda: pool.wait_ge(s_filled, 16 * (ECHUNKS + 2)))

        @block.scalar
        def _(act):
            a = nc.scalar
            act.wait_ge(s_setup_pe, 1)
            for l in range(LAYERS):
                a.copy(linT[:, 3 * l:3 * l + 3, :].rearrange("p m f -> p (m f)"), bank[l][:, 0:3 * P]
                       ).then_inc(s_setup_act, 1)
            act.wait_ge(s_consts, 6)

            for l in range(LAYERS):
                eb, base = ECHUNKS * l, CHUNKS * l
                if l:
                    act.wait_ge(s_gn, l)

                def normed(target, source):
                    if l == 0:
                        return a.copy(target, source)
                    return a.activation(target, source, ACT.Relu, bias=gn_bias[:, l - 1:l],
                                        scale=gn_scale[:, l - 1:l])

                def edge_gT(c):
                    wait(act, e_gT_psum, eb + c.n + 1)
                    wait(act, e_scan, eb + c.n - 1)
                    normed(gT[c.q], b_gT[c.q][:, :]).then_inc(e_gT, 1)

                def edge_keep(c):
                    wait(act, e_yT_psum, eb + c.n + 1)
                    a.copy(sums[:, bass.ds(c.n, 1), :].squeeze(1), b_back[:, :]).then_inc(e_y, 1)

                def nodes_xT(c):
                    for h in range(NODES):
                        n = c.n * NODES + h
                        wait(act, e_turned, base + n + 1)
                        wait(act, e_mm1, base + n - 1)
                        normed(xT[h], b_xT[h][:, :]).then_inc(e_xT, 1)

                sweep(act, ECHUNKS, [(2, edge_gT), (0, nodes_xT), (4, edge_keep)])

                def std(ready, var, sd, done, freed):
                    def stage(c):
                        if c.closes:
                            wait(act, ready, PAIRS * l + c.half + 1)
                            wait(act, freed, PAIRS * l + c.half - 1)
                            a.activation(sd[:, c.pair, :], var[:, c.pair, :], ACT.Sqrt, bias=epsc[:, 0:1],
                                         scale=1.0 / D).then_inc(done, 1)
                    return stage

                def relu(i, turned, source, target, freed, done):
                    def stage(c):
                        wait(act, turned, base + c.n + 1)
                        wait(act, freed, base + c.n - 3)
                        a.activation(target[c.q4], source[:, :], ACT.Relu, bias=col(LNB + 2 * l + i),
                                     scale=col(LNW + 2 * l + i)).then_inc(done, 1)
                    return stage

                def o_out(c):
                    wait(act, d_mm3, base + c.n + 1)
                    wait(act, s_store[c.q4], 16 * QUADS[c.q4] * l + quarter(c))
                    wait(act, d_ost, base + c.n - 3)
                    a.copy(o_rows[c.q4], b_3[c.q][:, :]).then_inc(d_o, 1)

                def norm2(c):
                    wait(act, d_r2, PAIRS * l + c.half + 1)
                    wait(act, d_n2T, base + c.n - 3)
                    for j in range(TILES):
                        last = a.activation(tile(n2[c.q4], j), tile(b_2[c.q4], j), ACT.Copy,
                                            scale=c.of_pair(r2)[:, j:j + 1])
                    last.then_inc(d_n2, 1)

                sweep(act, CHUNKS, [
                    (7, std(d_var2, var2, sd2, d_sd2, d_r2)), (2, std(d_var1, var1, sd1, d_sd1, d_r1)),
                    (5, relu(0, d_n1T, b_t1, h1T, d_mm2, d_h1)), (10, relu(1, d_n2T, b_t2, h2T, d_mm3, d_h2)),
                    (11, o_out), (8, norm2)], unroll=4)

                act.wait_ge(s_total_pe, 2 * l + 2)
                a.activation(tot[:, 4:5], bank[0][:, 1:2], ACT.Sqrt, bias=epsc[:, 0:1],
                             scale=1.0 / (N * D)).then_inc(s_total_act, 1)

            act.wait_ge(s_gn, LAYERS)
            act.wait_ge(s_inv, 1)

            def y_norm(c):
                wait(act, y_turned, c.n + 1)
                wait(act, y_back, c.n - 1)
                a.activation(xT[c.q], b_x[c.q][:, :], ACT.Relu, bias=gn_bias[:, LAYERS - 1:LAYERS],
                             scale=gn_scale[:, LAYERS - 1:LAYERS]).then_inc(y_xT, 1)

            def std(ready, var, sd, done, freed):
                def stage(c):
                    if c.closes:
                        wait(act, ready, c.half + 1)
                        wait(act, freed, c.half - 1)
                        a.activation(sd[:, c.pair, :], var[:, c.pair, :], ACT.Sqrt, bias=epsc[:, 0:1],
                                     scale=1.0 / D).then_inc(done, 1)
                return stage

            def scaled_rows(c, target, source, r, done):
                for j in range(TILES):
                    last = a.activation(tile(target, j), tile(source, j), ACT.Identity,
                                        bias=c.of_pair(shift)[:, j:j + 1], scale=c.of_pair(r)[:, j:j + 1])
                last.then_inc(done, 1)

            def y_out(c):
                wait(act, y_shift, c.half + 1)
                wait(act, y_store[c.q4], quarter(c))
                scaled_rows(c, y_rows[c.q4], z1[c.q4], r1, y_o)

            sweep(act, CHUNKS, [(1, y_norm), (3, std(y_var, var1, sd1, y_sd, y_r)), (5, y_out)], unroll=4)

            def m_gathered(c):
                wait(act, m_gT_psum, c.n + 1)
                wait(act, m_mm, c.n - 1)
                a.copy(gT[c.q], bank[c.q][:, :]).then_inc(m_gT, 1)

            def m_message(c):
                wait(act, m_mm, c.n + 1)
                wait(act, m_scan, c.n - 1)
                a.activation(msgT[c.q], bank[4 + c.q][:, :], ACT.Relu, bias=col(BMSG)).then_inc(m_msg, 1)

            sweep(act, ECHUNKS, [(0, m_gathered), (1, m_message)])

            def f_xT_out(c):
                wait(act, f_turned, c.n + 1)
                wait(act, f_z, c.n - 7)
                a.copy(x1T[c.q8], b_x[c.q][:, :]).then_inc(f_xT, 1)

            def f_norm(c):
                wait(act, f_r1, c.half + 1)
                wait(act, f_n1T, c.n - 1)
                for j in range(TILES):
                    last = a.activation(tile(n4[c.q], j), tile(s4[c.q4], j), ACT.Copy,
                                        scale=c.of_pair(r1)[:, j:j + 1])
                last.then_inc(f_n1, 1)

            def f_relu(c):
                wait(act, f_u, c.n + 1)
                wait(act, f_z, c.n - 1)
                a.activation(v4[c.q], u4[c.q], ACT.Relu, bias=col(BET)).then_inc(f_v, 1)

            def f_out(c):
                wait(act, f_shift, c.half + 1)
                wait(act, f_store[c.q4], quarter(c))
                scaled_rows(c, out_rows[c.q4], b_z[c.q4], r2, f_o)

            sweep(act, CHUNKS, [(3, std(f_var1, var1, sd1, f_sd1, f_r1)), (8, std(f_var2, var2, sd2, f_sd2, f_r2)),
                                (6, f_relu), (4, f_norm), (9, f_out), (0, f_xT_out)], unroll=8)

        @block.vector
        def _(dve):
            v = nc.vector
            dve.wait_ge(s_idx, 16 * 9)
            for source, target in ((src_i, src_f), (dst_i, dst_f), (nxt_i, nxt_f)):
                last = v.tensor_copy(target, source)
            chain = [0]

            def step(instruction):
                chain[0] += 1
                instruction.then_inc(s_chain, 1)
                dve.wait_ge(s_chain, chain[0])

            step(last)
            step(v.tensor_tensor(end_f, nxt_f, dst_f, ALU.is_lt))
            v.tensor_reduce(out=descents[:, 0:1], in_=end_f, axis=mybir.AxisListType.XY, op=ALU.add
                            ).then_inc(s_descents, 1)
            dve.wait_ge(s_descents_pe, 1)
            v.tensor_copy(unsorted[0:1, 0:1], bank[5][0:1, 0:1]).then_inc(s_unsorted, 1)

            def rank_tile(c):
                steps = [0]

                def follow(instruction):
                    steps[0] += 1
                    instruction.then_inc(o_step, 1)
                    dve.wait_ge(o_step, c.n * RANK_STEPS + (steps[0] + 2))

                own = same[:, bass.ds(c.n * P, P)]
                wait(dve, o_tile[c.q], 48 * (c.half + 1))
                follow(v.tensor_copy(dst_f32[:, c.q:c.q + 1], col_in[:, c.q, 1:2]))
                follow(v.tensor_copy(own, triangle))
                for k in range(PIECES):
                    part = slice(k * PIECE, (k + 1) * PIECE)
                    follow(v.scalar_tensor_tensor(out=goes_before[k % 2], in0=all_dst[:, part],
                                                  scalar=dst_f32[:, c.q:c.q + 1], in1=same[:, part],
                                                  op0=ALU.subtract, op1=ALU.is_lt))
                    follow(v.reduce_sum(rank_part[:, c.q, k:k + 1], goes_before[k % 2], axis=AXX))
                follow(v.reduce_sum(rank_part[:, c.q, PIECES:PIECES + 1], rank_part[:, c.q, 0:PIECES], axis=AXX))
                wait(dve, o_placed[c.q], 48 * c.half)
                v.tensor_copy(rank[:, c.q:c.q + 1], rank_part[:, c.q, PIECES:PIECES + 1]).then_inc(o_ranked, 1)
                follow(v.tensor_copy(own, ones[:, :]))

            dve.wait_ge(s_unsorted, 1)
            out_of_order = dve.value_load(unsorted[0:1, 0:1], min_val=0, max_val=E)
            with dve.If(out_of_order > 0):
                dve.wait_ge(o_all_dst, 16)
                v.tensor_copy(all_dst, all_dst.bitcast(I32)).then_inc(o_step, 1)
                v.memset(same[:, :], 0).then_inc(o_step, 1)
                dve.wait_ge(o_triangle, 1)
                dve.wait_ge(o_step, 2)
                sweep(dve, ETILES, [(0, rank_tile)])
                dve.wait_ge(s_idx, 16 * 18)
                for source, target in ((src_i, src_f), (dst_i, dst_f), (nxt_i, nxt_f)):
                    last = v.tensor_copy(target, source)
                last.then_inc(s_descents, 1)
                dve.wait_ge(s_descents, 2)
            with dve.Else():
                dve.wait_ge(s_unsorted, 1)
            step(v.tensor_tensor(end_f, dst_f, nxt_f, ALU.is_equal))
            v.tensor_copy(same_rows.rearrange("p (u e) -> p u e", u=2), end_f).then_inc(s_setup_dve, 1)
            dve.wait_ge(s_consts, 10)
            v.tensor_copy(thr, thr_i)
            step(v.tensor_scalar(spare_i, spare_i, SPARES - 1, None, ALU.bitwise_and))
            step(v.tensor_scalar(spare, spare_i, float(SPARE), None, ALU.add))
            step(v.tensor_tensor(spare, spare, dst_f, ALU.subtract))
            step(v.tensor_tensor(row_kept, spare, end_f, ALU.mult))
            v.tensor_tensor(end_f, row_kept, dst_f, ALU.add).then_inc(s_setup_dve, 1)
            for u in range(2):
                last = v.tensor_scalar(reach[:, u * P:u * P + CHUNKS], thr, dst_f[:, u, 0:1], None, ALU.is_gt)
            last.then_inc(s_setup_dve, 1)
            dve.wait_ge(s_setup_pe, 2)
            for u in range(2):
                v.tensor_copy(src_tab[:, u * HALF:(u + 1) * HALF], bank[3][:, u * P:u * P + HALF])
                v.tensor_copy(end_tab[:, u * HALF:(u + 1) * HALF], bank[3][:, (2 + u) * P:(2 + u) * P + HALF])
            v.tensor_copy(need_row[0:1, :], bank[5][0:1, 0:CHUNKS])
            v.tensor_copy(cols[:, :], bank[4][:, 0:P]).then_inc(s_setup_dve, 1)

            def copy_sources(c, turned, base):
                wait(dve, turned, base + c.n - 3)
                v.tensor_copy(src_now[:, c.q4, :], src_tab[:, bass.ds(c.n * TILES, TILES)]).then_inc(s_src_now, 1)

            def first_sources(turned, base):
                for n in range(4):
                    copy_sources(Chunk(n, n // 2, 0, n, True), turned, base)

            def next_sources(turned, base):
                def stage(c):
                    if not (c.fixed and c.n < 4):
                        copy_sources(c, turned, base)
                return stage

            dve.wait_ge(s_setup_dve, 4)
            first_sources(e_gT_psum, 0)
            dve.wait_ge(s_setup_act, LAYERS)
            dve.wait_ge(s_params, 16 * N_PARAMS)
            step(v.tensor_scalar(eps1[:, :], eps1[:, :], 1.0, None, ALU.add))
            step(v.reduce_sum(means9[:, 0:9], linT[:, :, :], axis=AXX))
            step(v.reduce_sum(means9[:, 9:11], w_upd[:, :, :], axis=AXX))
            step(v.reduce_sum(means9[:, 11:21], b_rows.rearrange("p (m f) -> p m f", f=D), axis=AXX))
            step(v.tensor_scalar(means9[:, 0:21], means9[:, 0:21], -1.0 / D, None, ALU.mult))
            for l in range(LAYERS):
                for i in range(2):
                    m = 3 * l + i
                    v.tensor_scalar(linT[:, m, :], linT[:, m, :], means9[:, m:m + 1], None, ALU.add)
                    last = v.tensor_scalar(b_rows[:, m * D:(m + 1) * D], b_rows[:, m * D:(m + 1) * D],
                                           means9[:, 11 + m:12 + m], None, ALU.add)
            for i in range(2):
                v.tensor_scalar(w_upd[:, i, :], w_upd[:, i, :], means9[:, 9 + i:10 + i], None, ALU.add)
            step(v.tensor_scalar(b_rows[:, 9 * D:10 * D], b_rows[:, 9 * D:10 * D], means9[:, 20:21], None, ALU.add))
            for l in range(LAYERS):
                v.tensor_scalar(lin1x[:, l, :], linT[:, 3 * l, :], eps1[:, l:l + 1], None, ALU.mult)
                v.tensor_copy(b_pre[:, l, :], b_rows[:, 3 * l * D:(3 * l + 1) * D])
            v.tensor_copy(b_pre[:, LAYERS, :], b_rows[:, 9 * D:10 * D])
            v.memset(tot[:, :], 0.0).then_inc(s_setup_dve, 1)
            dve.wait_ge(s_same_in, 16)

            def layer_norm_stages(base, mm, st, s_st, var, part, s_part, s_var, sd, s_sd, r, s_r, freed, source,
                                  mean=None):
                pairs = base // 2

                def stats(c):
                    if mm is not None:
                        wait(dve, mm, base + c.n + 1)
                    for j in range(TILES):
                        last = v.bn_stats(st[:, c.q4, j, :], tile(source(c), j))
                    last.then_inc(s_st, 1)

                def variance(c):
                    if not c.closes:
                        return
                    mean_e, m2_e, mean_o, m2_o = (
                        st[:, 2 * c.pair:2 * c.pair + 2, :, k].rearrange("p a j -> p (a j)") for k in (1, 2, 4, 5))
                    wait(dve, s_st, base + c.n + 1)
                    v.tensor_tensor(part[:, c.pair, 0, :], m2_e, m2_o, ALU.add)
                    if mean is None:
                        v.scalar_tensor_tensor(out=part[:, c.pair, 1, :], in0=mean_e, scalar=float(D), in1=mean_e,
                                               op0=ALU.mult, op1=ALU.mult).then_inc(s_part, 1)
                    else:
                        v.tensor_tensor(part[:, c.pair, 3, :], mean_e, mean_o, ALU.add)
                        v.tensor_tensor(part[:, c.pair, 2, :], mean_e, mean_o, ALU.subtract).then_inc(s_part, 1)
                        wait(dve, s_part, 2 * (pairs + c.half) + 1)
                        v.tensor_scalar(mean[:, c.pair, :], part[:, c.pair, 3, :], 0.5, None, ALU.mult)
                        v.scalar_tensor_tensor(out=part[:, c.pair, 1, :], in0=part[:, c.pair, 2, :], scalar=D / 4.0,
                                               in1=part[:, c.pair, 2, :], op0=ALU.mult, op1=ALU.mult
                                               ).then_inc(s_part, 1)
                    wait(dve, s_part, (1 if mean is None else 2) * (pairs + c.half + 1))
                    v.tensor_tensor(var[:, c.pair, :], part[:, c.pair, 0, :], part[:, c.pair, 1, :], ALU.add
                                    ).then_inc(s_var, 1)

                def inverse(c):
                    if c.closes:
                        wait(dve, s_sd, pairs + c.half + 1)
                        wait(dve, freed, base + c.n - 3)
                        v.reciprocal(r[:, c.pair, :], sd[:, c.pair, :]).then_inc(s_r, 1)
                return stats, variance, inverse

            def run_sum(ready, freed, done, base, source):
                def stage(c):
                    wait(dve, ready, base + c.n + 1)
                    wait(dve, freed, base + c.n - 1)
                    wait(dve, done, base + c.n)
                    first = 0.0 if c.is_(0) else yT[1 - c.q][:, ROWS - 1:ROWS]
                    v.tensor_tensor_scan(yT[c.q], same[:, bass.ds(c.n * ROWS, ROWS)], source[c.q], first,
                                         ALU.mult, ALU.add).then_inc(done, 1)
                return stage

            v.memset(fill[:, :], 0.0).then_inc(s_fill_row, 1)

            for l in range(LAYERS):
                eb, base = ECHUNKS * l, CHUNKS * l

                def nodes_pre(c):
                    for h in range(NODES):
                        n = c.n * NODES + h
                        wait(dve, e_mm1, base + n + 1)
                        r = c.q * NODES + h
                        wait(dve, s_pre_store[r], 16 * EVEN[c.q] * l + 16 * c.half)
                        v.tensor_tensor(tiles(pre_rows[r]), tiles(b_pre_rows[h][:, :]),
                                        b_pre[:, l:l + 1, :].to_broadcast([P, TILES, D]), ALU.add).then_inc(e_pre, 1)

                stages = [(0, next_sources(e_gT_psum, eb)), (4, run_sum(e_gT, e_yT_psum, e_scan, eb, gT)),
                          (3, nodes_pre)]
                if l == 0:
                    def edge_count(c):
                        wait(dve, s_count, c.n)
                        wait(dve, s_count_pe, c.n - 1)
                        first = 0.0 if c.is_(0) else count[1 - c.q][0:1, ROWS - 1:ROWS]
                        v.tensor_tensor_scan(count[c.q][0:1, :], same[0:1, bass.ds(c.n * ROWS, ROWS)], onerow[0:1, :],
                                             first, ALU.mult, ALU.add).then_inc(s_count, 1)
                    stages.append((4, edge_count))
                sweep(dve, ECHUNKS, stages, unroll=4)
                if l == 0:
                    step(v.memset(pick[:, :], 0.0))
                    for r in (0, 32, 64):
                        v.memset(pick[r:r + 1, :], 1.0)
                    step(v.memset(bias3[:, :, :], 0.0))
                    three = bias3[:, :, :].rearrange("p (l i) f -> p l (i f)", l=LAYERS)
                    left = b_rows[:, 0:9 * D].rearrange("p (l f) -> p l f", l=LAYERS)[:, :, D:3 * D]
                    for piece in range(3):
                        step(v.tensor_copy(b_bf, left))
                        last = v.tensor_copy(three[32 * piece:32 * piece + 32, :, :],
                                             b_bf[32 * piece:32 * piece + 32, :, :])
                        if piece < 2:
                            step(v.tensor_copy(b_part, b_bf))
                            step(v.tensor_tensor(left, left, b_part, ALU.subtract))
                    last.then_inc(s_setup_dve, 1)
                    dve.wait_ge(s_count_pe, ECHUNKS)
                    v.reciprocal(inv_tab[:, :], b_count[:, 0:ETILES]).then_inc(s_inv, 1)

                def pre_arrived(c):
                    wait(dve, s_aload[c.q4], 16 * QUADS[c.q4] * l + quarter(c) + 16)

                stats1, variance1, inverse1 = layer_norm_stages(
                    base, None, st1, d_st1, var1, part1, d_part1, d_var1, sd1, d_sd1, r1, d_r1, d_n1,
                    lambda c: node_in[c.q4])
                stats2, variance2, inverse2 = layer_norm_stages(
                    base, d_mm2, st2, d_st2, var2, part2, d_part2, d_var2, sd2, d_sd2, r2, d_r2, d_n2,
                    lambda c: b_2[c.q4][:, :])

                def norm1(c):
                    wait(dve, d_r1, PAIRS * l + c.half + 1)
                    wait(dve, d_n1T, base + c.n - 3)
                    v.tensor_tensor(tiles(n1[c.q4]), tiles(node_in[c.q4]),
                                    c.of_pair(r1).unsqueeze(2).to_broadcast([P, TILES, P]), ALU.mult
                                    ).then_inc(d_n1, 1)

                def out_stats(c):
                    wait(dve, d_o, base + c.n + 1)
                    v.bn_stats(st3[:, bass.ds(c.n, 1), :].squeeze(1), o_rows[c.q4]).then_inc(d_ost, 1)

                sweep(dve, CHUNKS, [(6, stats2), (1, pre_arrived), (1, stats1), (2, inverse1), (7, inverse2),
                                    (6, variance2), (13, out_stats), (3, norm1), (1, variance1)], unroll=4)

                if l < LAYERS - 1:
                    first_sources(e_gT_psum, ECHUNKS * (l + 1))

                dve.wait_ge(d_ost, base + CHUNKS)
                step(v.tensor_scalar(st3[:, CHUNKS - 1, :], st3[:, CHUNKS - 1, :], valid[:, 0:1], None, ALU.mult))
                mean_of = st3[:, :, :].rearrange("p c (h s) -> p c h s", s=3)[:, :, :, 1]
                m2_of = st3[:, :, :].rearrange("p c (h s) -> p c h s", s=3)[:, :, :, 2]
                v.tensor_copy(dev[:, :, :], mean_of)
                step(v.tensor_reduce(out=tot[:, 1:2], in_=m2_of, axis=mybir.AxisListType.XY, op=ALU.add))
                v.tensor_reduce(out=tot[:, 0:1], in_=dev[:, :, :], axis=mybir.AxisListType.XY, op=ALU.add
                                ).then_inc(s_total_act, 1)
                dve.wait_ge(s_total_pe, 2 * l + 1)
                step(v.tensor_scalar(tot[:, 2:3], bank[0][:, 0:1], -float(STATGROUP) / (N * D), None, ALU.mult))
                step(v.tensor_scalar(dev[:, :, :], dev[:, :, :], tot[:, 2:3], None, ALU.add))
                step(v.tensor_scalar(dev[:, CHUNKS - 1, :], dev[:, CHUNKS - 1, :], valid[:, 0:1], None, ALU.mult))
                step(v.tensor_tensor(dev[:, :, :], dev[:, :, :], dev[:, :, :], ALU.mult))
                step(v.tensor_reduce(out=tot[:, 3:4], in_=dev[:, :, :], axis=mybir.AxisListType.XY, op=ALU.add))
                v.scalar_tensor_tensor(out=tot[:, 3:4], in0=tot[:, 3:4], scalar=float(STATGROUP), in1=tot[:, 1:2],
                                       op0=ALU.mult, op1=ALU.add).then_inc(s_total_act, 1)
                dve.wait_ge(s_total_act, 3 * l + 3)
                step(v.reciprocal(tot[:, 5:6], tot[:, 4:5]))
                step(v.tensor_tensor(gn_scale[:, l:l + 1], tot[:, 5:6], col(OW + l), ALU.mult))
                v.scalar_tensor_tensor(out=gn_bias[:, l:l + 1], in0=tot[:, 2:3], scalar=gn_scale[:, l:l + 1],
                                       in1=col(OB + l), op0=ALU.mult, op1=ALU.add).then_inc(s_gn, 1)

            def y_sum(c):
                wait(dve, y_back, c.n + 1)
                wait(dve, y_xload[c.q4], quarter(c) + 16)
                wait(dve, y_o, c.n - 3)
                v.tensor_tensor(z1[c.q4], b_1[c.q4][:, :], x_in[c.q4], ALU.add).then_inc(y_z, 1)

            y_stats, y_vars, y_inverse = layer_norm_stages(
                0, y_z, st1, y_st, var1, part1, y_part, y_var, sd1, y_sd, r1, y_r, y_o, lambda c: z1[c.q4], mean1)

            def shift_stage(mean, r, s_r, done):
                def stage(c):
                    if c.closes:
                        wait(dve, s_r, c.half + 1)
                        v.scalar_tensor_tensor(out=shift[:, c.pair, :], in0=mean[:, c.pair, :], scalar=-1.0,
                                               in1=r[:, c.pair, :], op0=ALU.mult, op1=ALU.mult).then_inc(done, 1)
                return stage

            sweep(dve, CHUNKS, [(3, y_sum), (3, y_stats), (3, y_vars), (4, y_inverse),
                                (4, shift_stage(mean1, r1, y_r, y_shift))], unroll=4)

            def m_attrT(c):
                wait(dve, m_aT_psum, c.n + 1)
                wait(dve, m_mm, c.n - 1)
                v.tensor_copy(attrT[c.q], bank[2 + c.q][:, :]).then_inc(m_aT, 1)

            def m_keep(c):
                wait(dve, m_yT_psum, c.n + 1)
                for j in range(TILES):
                    last = v.scalar_tensor_tensor(
                        out=sums[:, bass.ds(c.n, 1), j * P:(j + 1) * P].squeeze(1), in0=tile(bank[6 + c.q], j),
                        scalar=inv_tab[:, bass.ds(c.n * TILES + j, 1)], in1=b_pre[:, LAYERS, :],
                        op0=ALU.mult, op1=ALU.add)
                last.then_inc(m_y, 1)

            first_sources(m_gT_psum, 0)
            dve.wait_ge(s_filled, 16 * 2)
            v.tensor_copy(fill[:, :].rearrange("p (r f) -> p r f", f=D),
                          b_pre[:, LAYERS:LAYERS + 1, :].to_broadcast([P, FILL // D, D])).then_inc(s_fill_row, 1)
            sweep(dve, ECHUNKS, [(0, next_sources(m_gT_psum, 0)), (3, m_attrT),
                                 (5, run_sum(m_msg, m_yT_psum, m_scan, 0, msgT)), (6, m_keep)], unroll=4)

            f_stats1, f_vars1, f_inverse1 = layer_norm_stages(
                0, f_sum, st1, f_st1, var1, part1, f_part1, f_var1, sd1, f_sd1, r1, f_r1, f_n1, lambda c: s4[c.q4])
            f_stats2, f_vars2, f_inverse2 = layer_norm_stages(
                0, f_z, st2, f_st2, var2, part2, f_part2, f_var2, sd2, f_sd2, r2, f_r2, f_o,
                lambda c: b_z[c.q4], mean2)

            def f_update(c):
                wait(dve, f_mm, c.n + 1)
                wait(dve, f_aload[c.q], 16 * (c.half + 1))
                wait(dve, f_n1, c.n - 3)
                v.tensor_tensor(s4[c.q4], b_p[:, :], a_in[:, c.q, :], ALU.add).then_inc(f_sum, 1)

            def f_residual(c):
                wait(dve, f_n1T, c.n + 1)
                wait(dve, f_v, c.n - 1)
                v.scalar_tensor_tensor(out=u4[c.q], in0=b_n[:, :], scalar=col(GAM), in1=x1T[c.q8],
                                       op0=ALU.mult, op1=ALU.add).then_inc(f_u, 1)

            sweep(dve, CHUNKS, [(2, f_update), (2, f_stats1), (2, f_vars1), (3, f_inverse1), (8, f_inverse2),
                                (8, shift_stage(mean2, r2, f_r2, f_shift)), (5, f_residual), (7, f_stats2),
                                (7, f_vars2)], unroll=8)

        @block.tensor
        def _(pe):
            t = nc.tensor

            def turn(target, source):
                for j in range(TILES):
                    last = t.transpose(tile(target, j), tile(source, j), ident[:, :])
                return last

            def linear(target, hT, weights, bias=None):
                if bias is not None:
                    t.matmul(tiles(target[:, :]), pick[:, :],
                             bias3[:, bias, :].unsqueeze(1).to_broadcast([P, TILES, D]), start=True, stop=False)
                for j in range(TILES):
                    last = t.matmul(tile(target, j), tile(hT, j), weights, start=bias is None,
                                    stop=bias is None or j == TILES - 1)
                return last

            pe.wait_ge(s_consts, 10)
            pe.wait_ge(s_descents, 1)
            t.matmul(bank[5][0:1, 0:1], descents[:, 0:1], ones[:, 0:1], start=True, stop=True
                     ).then_inc(s_descents_pe, 1)
            pe.wait_ge(s_params, 16 * N_PARAMS)
            for m in range(9):
                last = t.transpose(bank[m // 3][:, (m % 3) * P:(m % 3 + 1) * P], w_rows[:, m * D:(m + 1) * D],
                                   ident[:, :])
            last.then_inc(s_setup_pe, 1)
            pe.wait_ge(s_setup_dve, 3)
            for u in range(2):
                t.transpose(bank[3][:, u * P:(u + 1) * P], src_f[:, u, :], ident[:, :])
                t.transpose(bank[3][:, (2 + u) * P:(3 + u) * P], end_f[:, u, :], ident[:, :])
            t.transpose(bank[4][:, 0:P], v_rows, ident[:, :])
            for u in range(2):
                last = t.matmul(bank[5][0:1, 0:CHUNKS], ones[:, 0:1], reach[:, u * P:u * P + CHUNKS],
                                start=(u == 0), stop=(u == 1))
            last.then_inc(s_setup_pe, 1)
            pe.wait_ge(s_setup_dve, 5)

            for l in range(LAYERS):
                eb, base = ECHUNKS * l, CHUNKS * l

                def edge_turn(c):
                    wait(pe, s_gath[c.q4], 64 * EQUADS[c.q4] * l + 64 * (c.fourth + 1))
                    wait(pe, e_gT, eb + c.n - 1)
                    turn(b_gT[c.q], gathered[c.q4]).then_inc(e_gT_psum, 1)

                def edge_back(c):
                    wait(pe, e_scan, eb + c.n + 1)
                    wait(pe, e_y, eb + c.n)
                    linear(b_back, yT[c.q], linT[:, 3 * l, :]).then_inc(e_yT_psum, 1)

                def nodes_turn(c):
                    for h in range(NODES):
                        n = c.n * NODES + h
                        r = c.q * NODES + h
                        wait(pe, s_hload[r], 16 * (EVEN[c.q] * l) + 16 * (c.half + 1))
                        wait(pe, e_xT, base + n - 1)
                        turn(b_xT[h], node_in[r]).then_inc(e_turned, 1)

                def nodes_mm1(c):
                    for h in range(NODES):
                        n = c.n * NODES + h
                        wait(pe, e_xT, base + n + 1)
                        wait(pe, e_pre, base + n - 1)
                        linear(b_pre_rows[h], xT[h], lin1x[:, l, :]).then_inc(e_mm1, 1)

                stages = [(2, edge_turn), (0, nodes_turn), (4, edge_back), (1, nodes_mm1)]
                if l == 0:
                    def count_turn(c):
                        wait(pe, s_count, c.n + 1)
                        for j in range(TILES):
                            last = t.matmul(b_count[:, bass.ds(c.n * TILES + j, 1)], tile(count[c.q], j)[0:1, :],
                                            ones[0:1, 0:1], start=True, stop=True)
                        last.then_inc(s_count_pe, 1)
                    stages.append((4, count_turn))
                wait(pe, s_gn, l)
                sweep(pe, ECHUNKS, stages, unroll=4)
                if l == 0:
                    pe.wait_ge(s_inv, 1)
                    pe.wait_ge(s_setup_dve, 6)
                pe.wait_ge(e_y, eb + ECHUNKS)

                def turn1(c):
                    wait(pe, d_n1, base + c.n + 1)
                    wait(pe, d_h1, base + c.n)
                    turn(b_t1, n1[c.q4]).then_inc(d_n1T, 1)

                def mm2(c):
                    wait(pe, d_h1, base + c.n + 1)
                    wait(pe, d_n2, base + c.n - 3)
                    linear(b_2[c.q4], h1T[c.q4], linT[:, 3 * l + 1, :], 2 * l).then_inc(d_mm2, 1)

                def turn2(c):
                    wait(pe, d_n2, base + c.n + 1)
                    wait(pe, d_h2, base + c.n)
                    turn(b_t2, n2[c.q4]).then_inc(d_n2T, 1)

                def mm3(c):
                    wait(pe, d_h2, base + c.n + 1)
                    wait(pe, d_o, base + c.n - 1)
                    linear(b_3[c.q], h2T[c.q4], linT[:, 3 * l + 2, :], 2 * l + 1).then_inc(d_mm3, 1)

                sweep(pe, CHUNKS, [(5, mm2), (9, turn2), (4, turn1), (10, mm3)], unroll=4)

                for k in range(2):
                    pe.wait_ge(s_total_act, 3 * l + 1 + k)
                    t.matmul(bank[0][:, k:k + 1], ones[:, :], tot[:, 3 * k:3 * k + 1], start=True, stop=True
                             ).then_inc(s_total_pe, 1)
            pe.wait_ge(s_gn, LAYERS)

            def y_turn(c):
                wait(pe, y_hload[c.q4], quarter(c) + 16)
                wait(pe, y_xT, c.n - 1)
                turn(b_x[c.q], y_in[c.q4]).then_inc(y_turned, 1)

            def y_turn_back(c):
                wait(pe, y_xT, c.n + 1)
                wait(pe, y_z, c.n - 3)
                turn(b_1[c.q4], xT[c.q]).then_inc(y_back, 1)

            sweep(pe, CHUNKS, [(0, y_turn), (2, y_turn_back)], unroll=4)

            def m_turn(c):
                wait(pe, m_attr[c.q], 16 * (c.half + (2 if c.is_(ECHUNKS - 1) else 1)))
                wait(pe, m_aT, c.n - 1)
                turn(bank[2 + c.q], attr_in[c.q]).then_inc(m_aT_psum, 1)
                wait(pe, s_gath[c.q4], 64 * EQUADS[c.q4] * LAYERS + 64 * (c.fourth + 1))
                wait(pe, m_gT, c.n - 1)
                turn(bank[c.q], gathered[c.q4]).then_inc(m_gT_psum, 1)

            def m_matmul(c):
                wait(pe, m_gT, c.n + 1)
                wait(pe, m_aT, c.n + 1)
                wait(pe, m_msg, c.n - 1)
                t.matmul(bank[4 + c.q][:, :], w_msg[:, 0, :], gT[c.q], start=True, stop=False)
                t.matmul(bank[4 + c.q][:, :], w_msg[:, 1, :], attrT[c.q], start=False, stop=True).then_inc(m_mm, 1)

            def m_back(c):
                wait(pe, m_scan, c.n + 1)
                wait(pe, m_y, c.n - 1)
                linear(bank[6 + c.q], yT[c.q], w_upd[:, 1, :]).then_inc(m_yT_psum, 1)

            pe.wait_ge(y_z, CHUNKS)
            sweep(pe, ECHUNKS, [(0, m_turn), (1, m_matmul), (2, m_back)], unroll=4)
            pe.wait_ge(m_y, ECHUNKS)

            def f_turn(c):
                wait(pe, f_hload[c.q], 16 * (c.half + 1))
                wait(pe, f_xT, c.n - 1)
                turn(b_x[c.q], h_in[:, c.q, :]).then_inc(f_turned, 1)

            def f_matmul(c):
                wait(pe, f_xT, c.n + 1)
                wait(pe, f_sum, c.n)
                linear(b_p, x1T[c.q8], w_upd[:, 0, :]).then_inc(f_mm, 1)

            def f_turn1(c):
                wait(pe, f_n1, c.n + 1)
                wait(pe, f_u, c.n)
                turn(b_n, n4[c.q]).then_inc(f_n1T, 1)

            def f_rows(c):
                wait(pe, f_v, c.n + 1)
                wait(pe, f_o, c.n - 3)
                for j in range(TILES):
                    t.matmul(tile(b_z[c.q4], j), tile(x1T[c.q8], j), ident[:, :], start=True, stop=False)
                    last = t.matmul(tile(b_z[c.q4], j), tile(v4[c.q], j), ident[:, :], start=False, stop=True)
                last.then_inc(f_z, 1)

            sweep(pe, CHUNKS, [(2, f_matmul), (5, f_turn1), (1, f_turn), (7, f_rows)], unroll=8)


_INS = ["x", "src", "dst", "edge_attr_128", "L0_gnn_W", "L0_gnn_b", "L0_gnn_mlp_ln_w", "L0_gnn_mlp_ln_b",
        "L0_gnn_eps", "L0_gnn_out_ln_w", "L0_gnn_out_ln_b", "L1_gnn_W_msg", "L1_gnn_b_msg", "L1_gnn_W_upd",
        "L1_gnn_b_upd", "L1_gnn_gamma", "L1_gnn_beta"]


def kernel(**inputs):
    import numpy as _np
    import concourse.bacc as _bacc
    from concourse import mybir as _mybir
    from concourse.bass_utils import run_bass_kernel_spmd as _run

    nc = _bacc.Bacc("TRN2", target_bir_lowering=False, num_devices=1)
    arrays, args = {}, []
    for name in _INS:
        a = _np.ascontiguousarray(inputs[name])
        arrays[f"in_{name}"] = a
        args.append(nc.dram_tensor(f"in_{name}", a.shape, _mybir.dt.from_np(a.dtype), kind="ExternalInput").ap())
    args.append(nc.dram_tensor("out_rows_dram", (N, D), F32, kind="ExternalOutput").ap())
    build(nc, *args)
    r = _run(nc, [arrays], core_ids=[0])
    return r.results[0]["out_rows_dram"]
```
